# Optimizing a Trainium2 kernel written in Bass

```python
import numpy as np
import jax
import jax.numpy as jnp

def _softmax(x, axis=-1):
    return jax.nn.softmax(x, axis=axis)

def _gelu(x):
    return jax.nn.gelu(x, approximate=True)

def _silu(x):
    return jax.nn.silu(x)

def _sigmoid(x):
    return jax.nn.sigmoid(x)

def _layernorm(x, axis=-1, eps=1e-05):
    m = jnp.mean(x, axis=axis, keepdims=True)
    v = jnp.var(x, axis=axis, keepdims=True)
    return (x - m) / jnp.sqrt(v + eps)

def _scatter_add(tgt, idx, src, axis=0):
    return tgt.at[idx].add(src)

def _segment_sum(src, seg, n):
    return jax.ops.segment_sum(src, seg, n)
kernel_name = 'mk_decoder_postln_d1_seqx_r4_ec4197'

def setup_inputs(seed: int=0):
    np.random.seed(seed)
    _w = jnp.asarray

    def _rec_inputs():
        import jax
        import jax.numpy as jnp
        _rk = jax.random.key(seed)
        x = -1.394e-06 + 0.9999 * jax.random.normal(jax.random.fold_in(_rk, 1), (4, 512, 256), jnp.float32)
        _lenS = 512 - jax.random.randint(jax.random.fold_in(_rk, 7), (4,), 0, max(1, 512 // 4) + 1, jnp.int32)
        _lenS2 = 1601 - jax.random.randint(jax.random.fold_in(_rk, 8), (4,), 0, max(1, 1601 // 4) + 1, jnp.int32)
        _ctx_1024P = jax.random.normal(jax.random.fold_in(_rk, 11), (4, 16, 256), jnp.float32)
        _ctx_1024c = jax.random.dirichlet(jax.random.fold_in(_rk, 511), 0.3 * jnp.ones((16,), jnp.float32), (4, 1601))
        _ctx_1024t = jnp.einsum('bsk,bkd->bsd', _ctx_1024c, _ctx_1024P)
        _ctx_1024t = _ctx_1024t * jax.lax.rsqrt(jnp.mean(jnp.square(_ctx_1024t)) + 1e-12) * 0.953939
        ctx_1024 = -0.000292821 + 1.00034 * (_ctx_1024t + 0.3 * jax.random.normal(jax.random.fold_in(_rk, 611), (4, 1601, 256), jnp.float32))
        _validS = jnp.arange(512)[None, :] < _lenS[:, None]
        _validS2 = jnp.arange(1601)[None, :] < _lenS2[:, None]
        _causal = jnp.tril(jnp.ones((512, 512), dtype=bool))
        mask_Bx1xSxS2_if1 = jnp.where(jnp.ones((4, 1, 512, 1601), dtype=bool), 1, 0).astype(jnp.int32)
        return (x, ctx_1024, mask_Bx1xSxS2_if1)
    x, ctx_1024, mask_Bx1xSxS2_if1 = _rec_inputs()

    def _L0_attn_setup():
        import jax, jax.numpy as jnp
        import numpy as np
        N_EMBD = 256
        BLOCK_SIZE = 512
        ATTN_SPAN = 64
        LN_EPS = 1e-05

        def _band_mask(T, span, dtype):
            ones = jnp.ones((T, T), dtype=dtype)
            return jnp.tril(ones, 0) * (1.0 - jnp.tril(ones, -span))

        def _layer_norm(h, w, b):
            mu = jnp.mean(h, axis=-1, keepdims=True)
            var = jnp.var(h, axis=-1, keepdims=True)
            return (h - mu) * jax.lax.rsqrt(var + LN_EPS) * w + b
        key = jax.random.key(seed)
        k_x, k_w, k_b, k_lw = jax.random.split(key, 4)
        B, T, C = (4, BLOCK_SIZE, N_EMBD)
        x = jax.random.normal(k_x, (B, T, C), dtype=jnp.float32)
        lim = 1.0 / np.sqrt(C)
        W_qkv = jax.random.uniform(k_w, (C, 3 * C), minval=-lim, maxval=lim, dtype=jnp.float32)
        b_qkv = jax.random.uniform(k_b, (3 * C,), minval=-lim, maxval=lim, dtype=jnp.float32)
        ln_w = jnp.ones((C,), dtype=jnp.float32)
        ln_b = jnp.zeros((C,), dtype=jnp.float32)
        return {'x': x, 'W_qkv': W_qkv, 'b_qkv': b_qkv, 'ln_w': ln_w, 'ln_b': ln_b}
    _L0_attn_all = _L0_attn_setup()
    _L0_attn_in = {k: v for k, v in _L0_attn_all.items() if k in ('W_qkv', 'b_qkv', 'ln_w', 'ln_b')}
    del _L0_attn_all

    def _L0_xattn_setup():
        import jax, jax.numpy as jnp
        import numpy as np
        D_MODEL = 256
        HEADS = 16
        HEAD_DIM = D_MODEL // HEADS
        B, S = (2, 512)
        key0 = jax.random.key(seed)
        ks = jax.random.split(key0, 8)
        inp = {'key': jax.random.normal(ks[0], (B, S, D_MODEL), dtype=jnp.float32), 'query': jax.random.normal(ks[1], (B, S, D_MODEL), dtype=jnp.float32), 'value': jax.random.normal(ks[2], (B, S, D_MODEL), dtype=jnp.float32), 'mask': jnp.ones((B, 1, S, S), dtype=jnp.int32), 'Wq': jax.random.normal(ks[3], (D_MODEL, D_MODEL), dtype=jnp.float32) * 0.02, 'Wk': jax.random.normal(ks[4], (D_MODEL, D_MODEL), dtype=jnp.float32) * 0.02, 'Wv': jax.random.normal(ks[5], (D_MODEL, D_MODEL), dtype=jnp.float32) * 0.02, 'Wo': jax.random.normal(ks[6], (D_MODEL, D_MODEL), dtype=jnp.float32) * 0.02, 'bo': jax.random.normal(ks[7], (D_MODEL,), dtype=jnp.float32) * 0.02}
        return inp
    _L0_xattn_all = _L0_xattn_setup()
    _L0_xattn_in = {k: v for k, v in _L0_xattn_all.items() if k in ('Wq', 'Wk', 'Wv', 'Wo', 'bo')}
    del _L0_xattn_all

    def _L0_ffn_setup():
        import jax, jax.numpy as jnp
        import numpy as np
        H = 256
        E = 64
        K = 8
        G = 8
        TOPK_GROUP = 4
        I_MOE = 128
        I_SHARED = 512
        SCALE = 2.5

        def relu2(x):
            return jnp.square(jax.nn.relu(x))

        def _route(xf, router_w, correction_bias):
            T = xf.shape[0]
            logits = xf @ router_w.T
            scores = jax.nn.sigmoid(logits)
            sfc = scores + correction_bias[None, :]
            grp = sfc.reshape(T, G, E // G)
            top2, _ = jax.lax.top_k(grp, 2)
            group_scores = top2.sum(-1)
            _, gidx = jax.lax.top_k(group_scores, TOPK_GROUP)
            gmask = jnp.zeros((T, G), sfc.dtype).at[jnp.arange(T)[:, None], gidx].set(1.0)
            emask = jnp.repeat(gmask, E // G, axis=1)
            masked = jnp.where(emask > 0, sfc, 0.0)
            _, tidx = jax.lax.top_k(masked, K)
            tw = jnp.take_along_axis(scores, tidx, axis=1)
            tw = tw / (tw.sum(-1, keepdims=True) + 1e-20)
            return (tidx, tw * SCALE)
        key = jax.random.key(seed)
        ks = jax.random.split(key, 7)
        x = jax.random.normal(ks[0], (2, 256, H), dtype=jnp.float32)
        router_w = jax.random.normal(ks[1], (E, H), dtype=jnp.float32) * 0.02
        correction_bias = jax.random.normal(ks[2], (E,), dtype=jnp.float32) * 0.01
        up_w = jax.random.normal(ks[3], (E, H, I_MOE), dtype=jnp.float32) * 0.02
        down_w = jax.random.normal(ks[4], (E, I_MOE, H), dtype=jnp.float32) * 0.02
        shared_up_w = jax.random.normal(ks[5], (H, I_SHARED), dtype=jnp.float32) * 0.02
        shared_down_w = jax.random.normal(ks[6], (I_SHARED, H), dtype=jnp.float32) * 0.02
        return {'x': x, 'router_w': router_w, 'correction_bias': correction_bias, 'up_w': up_w, 'down_w': down_w, 'shared_up_w': shared_up_w, 'shared_down_w': shared_down_w}
    _L0_ffn_all = _L0_ffn_setup()
    _L0_ffn_in = {k: v for k, v in _L0_ffn_all.items() if k in ('router_w', 'correction_bias', 'up_w', 'down_w', 'shared_up_w', 'shared_down_w')}
    del _L0_ffn_all
    return {'x': x, 'ctx_1024': ctx_1024, 'mask_Bx1xSxS2_if1': mask_Bx1xSxS2_if1, 'L0_attn_W_qkv': _L0_attn_in['W_qkv'], 'L0_attn_b_qkv': _L0_attn_in['b_qkv'], 'L0_attn_ln_w': _L0_attn_in['ln_w'], 'L0_attn_ln_b': _L0_attn_in['ln_b'], 'L0_xattn_Wq': _L0_xattn_in['Wq'], 'L0_xattn_Wk': _L0_xattn_in['Wk'], 'L0_xattn_Wv': _L0_xattn_in['Wv'], 'L0_xattn_Wo': _L0_xattn_in['Wo'], 'L0_xattn_bo': _L0_xattn_in['bo'], 'L0_ffn_router_w': _L0_ffn_in['router_w'], 'L0_ffn_correction_bias': _L0_ffn_in['correction_bias'], 'L0_ffn_up_w': _L0_ffn_in['up_w'], 'L0_ffn_down_w': _L0_ffn_in['down_w'], 'L0_ffn_shared_up_w': _L0_ffn_in['shared_up_w'], 'L0_ffn_shared_down_w': _L0_ffn_in['shared_down_w']}

def reference(x, ctx_1024, mask_Bx1xSxS2_if1, L0_attn_W_qkv, L0_attn_b_qkv, L0_attn_ln_w, L0_attn_ln_b, L0_xattn_Wq, L0_xattn_Wk, L0_xattn_Wv, L0_xattn_Wo, L0_xattn_bo, L0_ffn_router_w, L0_ffn_correction_bias, L0_ffn_up_w, L0_ffn_down_w, L0_ffn_shared_up_w, L0_ffn_shared_down_w):
    import jax
    import jax.numpy as jnp

    def _L0_attn_ref(x, W_qkv, b_qkv, ln_w, ln_b):
        import jax, jax.numpy as jnp
        import numpy as np
        N_EMBD = 256
        BLOCK_SIZE = 512
        ATTN_SPAN = 64
        LN_EPS = 1e-05

        def _band_mask(T, span, dtype):
            ones = jnp.ones((T, T), dtype=dtype)
            return jnp.tril(ones, 0) * (1.0 - jnp.tril(ones, -span))

        def _layer_norm(h, w, b):
            mu = jnp.mean(h, axis=-1, keepdims=True)
            var = jnp.var(h, axis=-1, keepdims=True)
            return (h - mu) * jax.lax.rsqrt(var + LN_EPS) * w + b
        B, T, C = x.shape
        qkv = x @ W_qkv + b_qkv
        q, k, v = jnp.split(qkv, 3, axis=-1)
        scale = np.sqrt(C * ATTN_SPAN).astype(np.float32)
        scores = jnp.einsum('bid,bjd->bij', q, k) / scale
        scores = scores * _band_mask(T, ATTN_SPAN, x.dtype)[None, :, :]
        out = jnp.einsum('bij,bjd->bid', scores, v)
        return _layer_norm(out, ln_w, ln_b)

    def _L0_xattn_ref(key, query, value, mask, Wq, Wk, Wv, Wo, bo):
        import jax, jax.numpy as jnp
        import numpy as np
        D_MODEL = 256
        HEADS = 16
        HEAD_DIM = D_MODEL // HEADS
        B, S = (2, 512)
        b, q_len, d = query.shape
        k_len = key.shape[1]
        h, hd = (HEADS, HEAD_DIM)
        q = (query @ Wq.T).reshape(b, q_len, h, hd)
        k = (key @ Wk.T).reshape(b, k_len, h, hd)
        v = (value @ Wv.T).reshape(b, k_len, h, hd)
        product = jnp.einsum('bqhd,bkhd->bhqk', q, k)
        product = jnp.where(mask == 0, jnp.float32(-1e+20), product)
        product = product / jnp.sqrt(jnp.asarray(hd, product.dtype))
        scores = jax.nn.softmax(product, axis=-1)
        out = jnp.einsum('bhqk,bkhd->bqhd', scores, v).reshape(b, q_len, h * hd)
        return out @ Wo.T + bo

    def _L0_ffn_ref(x, router_w, correction_bias, up_w, down_w, shared_up_w, shared_down_w):
        import jax, jax.numpy as jnp
        import numpy as np
        H = 256
        E = 64
        K = 8
        G = 8
        TOPK_GROUP = 4
        I_MOE = 128
        I_SHARED = 512
        SCALE = 2.5

        def relu2(x):
            return jnp.square(jax.nn.relu(x))

        def _route(xf, router_w, correction_bias):
            T = xf.shape[0]
            logits = xf @ router_w.T
            scores = jax.nn.sigmoid(logits)
            sfc = scores + correction_bias[None, :]
            grp = sfc.reshape(T, G, E // G)
            top2, _ = jax.lax.top_k(grp, 2)
            group_scores = top2.sum(-1)
            _, gidx = jax.lax.top_k(group_scores, TOPK_GROUP)
            gmask = jnp.zeros((T, G), sfc.dtype).at[jnp.arange(T)[:, None], gidx].set(1.0)
            emask = jnp.repeat(gmask, E // G, axis=1)
            masked = jnp.where(emask > 0, sfc, 0.0)
            _, tidx = jax.lax.top_k(masked, K)
            tw = jnp.take_along_axis(scores, tidx, axis=1)
            tw = tw / (tw.sum(-1, keepdims=True) + 1e-20)
            return (tidx, tw * SCALE)
        B, S, Hd = x.shape
        xf = x.reshape(-1, Hd)
        T = xf.shape[0]
        tidx, tw = _route(xf.astype(jnp.float32), router_w, correction_bias)
        combine = jnp.zeros((T, E), xf.dtype).at[jnp.arange(T)[:, None], tidx].add(tw.astype(xf.dtype))

        def body(acc, ew):
            wu, wd, c = ew
            return (acc + c[:, None] * (relu2(xf @ wu) @ wd), None)
        routed, _ = jax.lax.scan(body, jnp.zeros_like(xf), (up_w, down_w, combine.T))
        shared = relu2(xf @ shared_up_w) @ shared_down_w
        return (routed + shared).reshape(B, S, Hd)
    x = _layernorm(x + _L0_attn_ref(x, L0_attn_W_qkv, L0_attn_b_qkv, L0_attn_ln_w, L0_attn_ln_b), axis=-1)
    x = _layernorm(x + _L0_xattn_ref(ctx_1024, x, ctx_1024, mask_Bx1xSxS2_if1, L0_xattn_Wq, L0_xattn_Wk, L0_xattn_Wv, L0_xattn_Wo, L0_xattn_bo), axis=-1)
    x = _layernorm(x + _L0_ffn_ref(x, L0_ffn_router_w, L0_ffn_correction_bias, L0_ffn_up_w, L0_ffn_down_w, L0_ffn_shared_up_w, L0_ffn_shared_down_w), axis=-1)
    return x

_drawn_inputs = setup_inputs


def setup_inputs(seed=0):
    import zlib

    import numpy as np

    out = dict(_drawn_inputs(seed))
    spreads = {'L0_attn_ln_w': (1.0, 0.2), 'L0_attn_ln_b': (0.0, 0.1)}
    factors = {'L0_xattn_Wq': 8.0,
     'L0_xattn_Wk': 8.0,
     'L0_xattn_bo': 2.741,
     'L0_ffn_correction_bias': 6.347}
    for name, (base, spread) in spreads.items():
        noise = np.random.default_rng([zlib.crc32(name.encode()), seed]).standard_normal(out[name].shape)
        drawn = base * np.exp(spread * noise) if base else spread * noise
        out[name] = jnp.asarray(drawn.astype(out[name].dtype))
    for name, factor in factors.items():
        out[name] = (out[name] * factor).astype(out[name].dtype)
    return out
```

```python
import concourse.bass as bass
from concourse import mybir
from contextlib import ExitStack

F32, BF16, I32 = mybir.dt.float32, mybir.dt.bfloat16, mybir.dt.int32
ALU, ACT, AX = mybir.AluOpType, mybir.ActivationFunctionType, mybir.AxisListType

P = 128
B, T, D = 4, 512, 256
S2 = 1601
H, HD = 16, 16
SPAN = 64
E, I_MOE, I_SHARED = 64, 128, 512
EXPERTS = E + I_SHARED // I_MOE
G, TOPK_GROUP, K_TOP = 8, 4, 8
ROUTE_SCALE = 2.5
EPS = 1e-5
MASKED = -1e20
LOWEST = -1e30

DC = D // P
TT = T // P
NT = B * TT
KT = -(-S2 // P)
KW = [min(P, S2 - P * k) for k in range(KT)]
CHUNKS = [(c, min(512, S2 - c)) for c in range(0, S2, 512)]
GH = 4
NG = H // GH
TERMS = [(0, 0), (0, 1), (1, 0), (1, 1), (0, 2), (2, 0)]
ROWS = len(TERMS) * HD
MROWS = 3
HALF = 1024


def semaphores(ctx, nc, names):
    return {n: ctx.enter_context(nc.semaphore(n)) for n in names.split()}


def as_range(sems):
    numbers = sorted(s.num for s in sems)
    assert numbers == list(range(numbers[0], numbers[0] + len(numbers)))
    return range(numbers[0], numbers[-1] + 1)


def decoder_layer(nc, x, xT, ctxT, mask, w_qkv, b_qkv, ln_w, ln_b, wqT, wkT, wvT, woT, bo,
                  router_wT, correction, up_w, down_w, out):
    k_parts_dram = nc.dram_tensor("k_parts_dram", (3, D, S2), BF16).ap()
    q_parts_dram = nc.dram_tensor("q_parts_dram", (3, D, T), BF16).ap()

    with ExitStack() as ctx:
        def sb(name, shape, dt=F32, c=ctx):
            return c.enter_context(nc.sbuf_tensor(name, shape, dt))

        x2 = sb("x2", [P, NT, D])
        ident = sb("ident", [P, P])
        ident_bf = sb("ident_bf", [P, P], BF16)
        ps = ctx.enter_context(nc.psum_tensor("ps", [P, 8, 512], F32))

        attention(nc, x2, ident, ident_bf, ps, k_parts_dram, q_parts_dram, x, xT, ctxT, mask,
                  w_qkv, b_qkv, ln_w, ln_b, wqT, wkT, wvT, woT, bo)
        mixture(nc, x2, ident, ps, router_wT, correction, up_w, down_w, out)


def attention(nc, x2, ident, ident_bf, ps, k_parts_dram, q_parts_dram, x, xT, ctxT, mask,
              w_qkv, b_qkv, ln_w, ln_b, wqT, wkT, wvT, woT, bo):
    with ExitStack() as ctx:
        def sb(name, shape, dt=F32):
            return ctx.enter_context(nc.sbuf_tensor(name, shape, dt))

        band = sb("band", [P, 2 * P])
        w_qkv_sb = sb("w_qkv_sb", [P, DC, 3 * D])
        wq_sb = sb("wq_sb", [P, DC, D])
        wk_sb = sb("wk_sb", [P, DC, D])
        wv_sb = sb("wv_sb", [P, DC, D])
        wo_sb = sb("wo_sb", [P, DC, D])
        qk_bias = sb("qk_bias", [P, 2 * DC])
        v_bias = sb("v_bias", [P, D])
        lnw_sb = sb("lnw_sb", [P, D])
        lnb_sb = sb("lnb_sb", [P, D])
        bo_sb = sb("bo_sb", [P, D])
        power = sb("power", [P, TT])

        k_aug = sb("k_aug", [ROWS + MROWS, 2, GH, S2], BF16)
        q_aug = sb("q_aug", [ROWS + MROWS, H, T], BF16)
        v_aug = sb("v_aug", [P, KT, H, 2 * HD])
        k_parts = sb("k_parts", [P, 3, DC, S2], BF16)
        q_parts = sb("q_parts", [P, 3, DC, T], BF16)
        bias = sb("bias", [P, TT, S2], BF16)

        early = sb("early", [P, 4, S2])
        ctx_sb = early[:, 0:2, :]
        mask_sb = early[:, 2:4, :].bitcast(I32)
        PRING = 8
        probs = early[:, :, :].rearrange("p a b -> p (a b)")[:, 0:PRING * T].rearrange(
            "p (s t) -> p s t", t=T)

        shared = sb("shared", [P, 8, 512])
        qk_sb = shared[:, 0:4, :]
        v_sb = shared[:, 4:6, :].rearrange("p a b -> p (a b)").rearrange("p (t d) -> p t d", t=TT)
        st_sb = shared[:, 6:8, :].rearrange("p a b -> p (a b)").rearrange("p (t d) -> p t d", t=TT)
        oT_sb = shared[:, 0:4, :]
        on_sb = v_sb
        onT_sb = shared[:, 6:8, :]

        xT_sb = sb("xT_sb", [P, DC, T])
        x1T_sb = xT_sb
        x_sb = sb("x_sb", [P, TT, D])
        u_sb = sb("u_sb", [P, TT, D])
        x1_sb = sb("x1_sb", [P, TT, D])
        rest = sb("rest", [P, 2, 512])
        junk = sb("junk", [P, S2], BF16)
        stats = sb("stats", [P, TT, 6])
        mv = sb("mv", [P, TT, 2])
        ve = sb("ve", [P, TT])
        rstd = sb("rstd", [P, TT])
        mx = sb("mx", [P, 2, TT, GH])
        m_full = sb("m_full", [P, TT, GH])
        m_rest = sb("m_rest", [P, TT, GH])
        m_parts = sb("m_parts", [P, TT, GH, MROWS], BF16)
        rsum = sb("rsum", [P, TT, H])

        once = semaphores(ctx, nc, "s_weights s_ident0 s_ident s_const s_ones")
        s_weights, s_ident0, s_ident, s_const, s_ones = once.values()

        with nc.Block(no_gpsimd_drain=True) as block:
            @block.sync
            def _(sp):
                for dst, src in ((w_qkv_sb, w_qkv), (wq_sb, wqT), (wk_sb, wkT), (wv_sb, wvT), (wo_sb, woT)):
                    sp.dma_start(dst[:], src.rearrange("(c p) n -> p c n", p=P)).then_inc(s_weights, 16)
                with nc.allow_non_contiguous_dma(reason="512 bias values, once"):
                    sp.dma_start(qk_bias[:], b_qkv[0:2 * D].rearrange("(c p) -> p c", p=P)).then_inc(s_weights, 16)
                for dst, src in ((v_bias, b_qkv[2 * D:3 * D]), (lnw_sb, ln_w), (lnb_sb, ln_b), (bo_sb, bo)):
                    sp.dma_start(dst[:], src.rearrange("(a n) -> a n", a=1).to_broadcast([P, D])).then_inc(s_weights, 16)
                sp.wait_ge(s_weights, 16 * 10)

            @block.gpsimd
            def _(pool):
                nc.gpsimd.memset(ident[:], 0.0).then_inc(s_ident0, 1)
                nc.gpsimd.memset(band[:], 1.0 / (D * SPAN) ** 0.5).then_inc(s_ident0, 1)
                nc.gpsimd.memset(power[:], -0.5).then_inc(s_ident0, 1)
                pool.wait_ge(s_ident0, 2)
                nc.gpsimd.affine_select(out=ident[:], in_=ident[:], compare_op=ALU.not_equal, fill=1.0,
                                        base=0, pattern=[[-1, P]], channel_multiplier=1).then_inc(s_ident, 1)
                nc.gpsimd.affine_select(out=band[:], in_=band[:], compare_op=ALU.is_ge, fill=0.0,
                                        base=0, pattern=[[1, 2 * P]], channel_multiplier=-1).then_inc(s_const, 1)
                pool.wait_ge(s_const, 1)
                nc.gpsimd.affine_select(out=band[:], in_=band[:], compare_op=ALU.is_ge, fill=0.0,
                                        base=SPAN - 1, pattern=[[-1, 2 * P]], channel_multiplier=1).then_inc(s_const, 1)
                pool.wait_ge(s_const, 2)

            @block.vector
            def _(dve):
                nc.vector.memset(v_aug[:], 1.0).then_inc(s_ones, 1)
                nc.vector.memset(k_aug[ROWS:ROWS + MROWS, :, :, :], 1.0).then_inc(s_ones, 1)
                dve.wait_ge(s_ident, 1)
                nc.vector.tensor_copy(ident_bf[:], ident[:]).then_inc(s_ones, 1)
                dve.wait_ge(s_ones, 3)

        per_batch = semaphores(
            ctx, nc,
            "s_x s_ctx s_mask0 s_mask1 s_bias s_qk s_qk_sb s_v s_v_sb s_band s_band_sb s_o s_rest "
            "s_var s_rstd s_x1 s_x1T s_x1T_sb s_pr s_p1 s_p2 s_p3 s_vx s_vx_sb s_vx_sb2 s_dve s_pool "
            "s_kd s_qd s_kl0 s_kl1 s_ql s_sA s_sB s_mA s_mB s_mp s_mT s_mr s_st s_exp s_pv s_oT s_oTs "
            "s_tr s_on s_tr2 s_onT s_y s_xdone")
        S = per_batch
        s_mask = [S["s_mask0"], S["s_mask1"]]
        s_kl = [S["s_kl0"], S["s_kl1"]]

        def norm(link, dve, base, src, dst, first):
            for t in range(TT):
                nc.vector.bn_stats(stats[:, t, :], src(t)).then_inc(S["s_dve"], 1)
                link.n += 1
            dve.wait_ge(S["s_dve"], link.n)
            for t in range(TT):
                nc.vector.bn_aggr(mv[:, t, :], stats[:, t, :]).then_inc(S["s_dve"], 1)
                link.n += 1
            dve.wait_ge(S["s_dve"], link.n)
            nc.vector.tensor_scalar(ve[:], mv[:, :, 1], EPS, None, ALU.add).then_inc(S["s_var"], 1)
            dve.wait_ge(S["s_rstd"], base + 1)
            for t in range(TT):
                nc.vector.tensor_scalar(dst(t), src(t), mv[:, t, 0:1], rstd[:, t:t + 1],
                                        ALU.subtract, ALU.mult).then_inc(S["s_dve"], 1)
                link.n += 1
            dve.wait_ge(S["s_dve"], link.n)

        class Link:
            def __init__(self, dve):
                self.dve, self.n = dve, 0

            def __call__(self, ins):
                self.n += 1
                ins.then_inc(S["s_dve"], 1)
                self.dve.wait_ge(S["s_dve"], self.n)

        def bank(i):
            return ps[:, i, :]

        def bcast_rows(ap, n):
            return ap.rearrange("p (a d) -> p a d", a=1).to_broadcast([P, n, ap.shape[1]])

        PROJ = [(False, m, c, w) for m in range(DC) for c, w in CHUNKS] + [(True, m, 0, T) for m in range(DC)]
        NK = DC * len(CHUNKS)

        def proj_bank(n):
            return n % 4 if n < NK else 6 + n - NK

        def load_k(sp, g):
            for i, (_, tk) in enumerate(TERMS):
                sp.dma_start(k_aug[i * HD:(i + 1) * HD, g % 2, :, :],
                             k_parts_dram[tk, g * GH * HD:(g + 1) * GH * HD, :].rearrange(
                                 "(h p) n -> p h n", p=HD)).then_inc(s_kl[g % 2], 16)

        with nc.Fori(0, B) as b:
            with nc.Block(no_gpsimd_drain=True) as block:
                @block.sync
                def _(sp):
                    sp.dma_start(xT_sb[:], xT[:, bass.ds(b * T, T)].rearrange("(c p) t -> p c t", p=P)).then_inc(S["s_x"], 16)
                    sp.dma_start(ctx_sb, ctxT[bass.ds(b * D, D), :].rearrange("(c p) n -> p c n", p=P)).then_inc(S["s_ctx"], 16)
                    sp.dma_start(x_sb[:], x[bass.ds(b * T, T), :].rearrange("(t p) d -> p t d", p=P)).then_inc(S["s_x"], 16)
                    for t in range(TT):
                        if t >= 2:
                            sp.wait_ge(S["s_bias"], t - 1)
                        sp.dma_start(mask_sb[:, t % 2, :], mask[bass.ds(b * T + t * P, P), :]).then_inc(s_mask[t % 2], 16)
                    sp.wait_ge(S["s_p3"], NK)
                    sp.wait_ge(S["s_p2"], NK)
                    for m in range(DC):
                        sp.dma_start(k_parts_dram[:, m * P:(m + 1) * P, :].rearrange("t p n -> p t n"),
                                     k_parts[:, :, m, :]).then_inc(S["s_kd"], 16)
                    sp.wait_ge(S["s_kd"], 16 * DC)
                    for g in range(2):
                        load_k(sp, g)
                    sp.wait_ge(S["s_p3"], NK + DC)
                    sp.wait_ge(S["s_p2"], NK + DC)
                    for m in range(DC):
                        sp.dma_start(q_parts_dram[:, m * P:(m + 1) * P, :].rearrange("t p n -> p t n"),
                                     q_parts[:, :, m, :]).then_inc(S["s_qd"], 16)
                    sp.wait_ge(S["s_qd"], 16 * DC)
                    for i, (tq, _) in enumerate(TERMS):
                        sp.dma_start(q_aug[i * HD:(i + 1) * HD, :, :],
                                     q_parts_dram[tq].rearrange("(h p) n -> p h n", p=HD)).then_inc(S["s_ql"], 16)

                @block.tensor
                def _(pe):
                    pe.wait_ge(S["s_x"], 32)
                    for m in range(2 * DC):
                        for c in range(DC):
                            last = nc.tensor.matmul(bank(m), w_qkv_sb[:, c, m * P:(m + 1) * P], xT_sb[:, c, :],
                                                    start=(c == 0), stop=(c == DC - 1))
                        last.then_inc(S["s_qk"], 1)
                    for t in range(TT):
                        for c in range(DC):
                            last = nc.tensor.matmul(ps[:, 4 + t, 0:D], xT_sb[:, c, t * P:(t + 1) * P],
                                                    w_qkv_sb[:, c, 2 * D:3 * D], start=(c == 0), stop=(c == DC - 1))
                        last.then_inc(S["s_v"], 1)
                    pe.wait_ge(S["s_qk_sb"], 2 * DC)
                    for t in range(TT):
                        w = min(2 * P, T - t * P)
                        for c in range(DC):
                            last = nc.tensor.matmul(ps[:, t, 0:w], qk_sb[:, DC + c, t * P:(t + 1) * P],
                                                    qk_sb[:, c, t * P:t * P + w], start=(c == 0), stop=(c == DC - 1))
                        last.then_inc(S["s_band"], 1)
                    pe.wait_ge(S["s_v_sb"], TT)
                    for t in range(TT):
                        pe.wait_ge(S["s_band_sb"], t + 1)
                        last = nc.tensor.matmul(ps[:, 4 + t, 0:D], st_sb[:, t, 0:P], v_sb[:, t, :],
                                                start=True, stop=(t == 0))
                        if t:
                            last = nc.tensor.matmul(ps[:, 4 + t, 0:D], st_sb[:, t - 1, P:2 * P], v_sb[:, t - 1, :],
                                                    start=False, stop=True)
                        last.then_inc(S["s_o"], 1)
                    pe.wait_ge(S["s_ctx"], 16)
                    for n in range(NK):
                        _, m, c0, w = PROJ[n]
                        if n >= 4:
                            pe.wait_ge(S["s_rest"], n - 3)
                        for c in range(DC):
                            last = nc.tensor.matmul(ps[:, proj_bank(n), 0:w], wk_sb[:, c, m * P:(m + 1) * P],
                                                    ctx_sb[:, c, c0:c0 + w], start=(c == 0), stop=(c == DC - 1))
                        last.then_inc(S["s_pr"], 1)
                    for k in range(KT):
                        if k < 4:
                            pe.wait_ge(S["s_rest"], NK - 3 + k)
                        else:
                            pe.wait_ge(S["s_vx_sb"], k - 3)
                        for c in range(DC):
                            last = nc.tensor.matmul(ps[0:KW[k], k % 4, 0:D], ctx_sb[:, c, k * P:k * P + KW[k]],
                                                    wv_sb[:, c, :], start=(c == 0), stop=(c == DC - 1))
                        last.then_inc(S["s_vx"], 1)
                    pe.wait_ge(S["s_x1"], 1)
                    for c in range(DC):
                        for t in range(TT):
                            last = nc.tensor.transpose(ps[:, 4 + c, t * P:(t + 1) * P], x1_sb[:, t, c * P:(c + 1) * P], ident[:])
                        last.then_inc(S["s_x1T"], 1)
                    pe.wait_ge(S["s_x1T_sb"], DC)
                    for n in range(NK, NK + DC):
                        m = PROJ[n][1]
                        for c in range(DC):
                            last = nc.tensor.matmul(bank(proj_bank(n)), wq_sb[:, c, m * P:(m + 1) * P], x1T_sb[:, c, :],
                                                    start=(c == 0), stop=(c == DC - 1))
                        last.then_inc(S["s_pr"], 1)

                def parts_of(n):
                    is_q, m, c0, w = PROJ[n]
                    return (q_parts if is_q else k_parts), m, c0, w

                @block.scalar
                def _(act):
                    for m in range(2 * DC):
                        act.wait_ge(S["s_qk"], m + 1)
                        nc.scalar.activation(qk_sb[:, m, :], bank(m), ACT.Identity, bias=qk_bias[:, m:m + 1]).then_inc(S["s_qk_sb"], 1)

                    def first(n):
                        parts, m, c0, w = parts_of(n)
                        act.wait_ge(S["s_pr"], n + 1)
                        nc.scalar.copy(parts[:, 0, m, c0:c0 + w], ps[:, proj_bank(n), 0:w]).then_inc(S["s_p1"], 1)

                    def second(n):
                        parts, m, c0, w = parts_of(n)
                        act.wait_ge(S["s_rest"], n + 1)
                        nc.scalar.copy(parts[:, 1, m, c0:c0 + w], rest[:, n % 2, 0:w]).then_inc(S["s_p2"], 1)

                    for n in range(NK):
                        first(n)
                        if n:
                            second(n - 1)
                    second(NK - 1)
                    for k in range(KT):
                        act.wait_ge(S["s_vx"], k + 1)
                        nc.scalar.copy(v_aug[0:KW[k], k, :, 0:HD],
                                       ps[0:KW[k], k % 4, 0:D].rearrange("p (h d) -> p h d", h=H)).then_inc(S["s_vx_sb"], 1)
                    for c in range(DC):
                        act.wait_ge(S["s_x1T"], c + 1)
                        nc.scalar.copy(x1T_sb[:, c, :], bank(4 + c)).then_inc(S["s_x1T_sb"], 1)
                    first(NK)
                    first(NK + 1)
                    second(NK)
                    second(NK + 1)

                @block.gpsimd
                def _(pool):
                    def rsqrt(n):
                        pool.wait_ge(S["s_var"], n + 1)
                        nc.gpsimd.tensor_tensor(rstd[:], ve[:], power[:], ALU.pow).then_inc(S["s_rstd"], 1)

                    def mask_tile(t):
                        pool.wait_ge(s_mask[t % 2], 16 * (t // 2 + 1))
                        nc.gpsimd.tensor_scalar(bias[:, t, :], mask_sb[:, t % 2, :], 0.0, MASKED,
                                                ALU.is_equal, ALU.mult).then_inc(S["s_bias"], 1)

                    def third(n):
                        parts, m, c0, w = parts_of(n)
                        pool.wait_ge(S["s_p2"], n + 1)
                        nc.gpsimd.tensor_tensor(parts[:, 2, m, c0:c0 + w], rest[:, n % 2, 0:w],
                                                parts[:, 1, m, c0:c0 + w], ALU.subtract).then_inc(S["s_p3"], 1)

                    mask_tile(0)
                    rsqrt(0)
                    rsqrt(1)
                    for n in range(NK):
                        third(n)
                    for t in range(1, TT):
                        mask_tile(t)
                    third(NK)
                    third(NK + 1)

                @block.vector
                def _(dve):
                    link = Link(dve)
                    for t in range(TT):
                        dve.wait_ge(S["s_v"], t + 1)
                        nc.vector.tensor_tensor(v_sb[:, t, :], ps[:, 4 + t, 0:D], v_bias[:], ALU.add).then_inc(S["s_v_sb"], 1)
                    for t in range(TT):
                        w = min(2 * P, T - t * P)
                        dve.wait_ge(S["s_band"], t + 1)
                        nc.vector.tensor_tensor(st_sb[:, t, 0:w], ps[:, t, 0:w], band[:, 0:w], ALU.mult).then_inc(S["s_band_sb"], 1)
                    dve.wait_ge(S["s_o"], TT)
                    norm(link, dve, 0, lambda t: ps[:, 4 + t, 0:D], lambda t: u_sb[:, t, :], True)
                    link(nc.vector.tensor_tensor(u_sb[:], u_sb[:], bcast_rows(lnw_sb[:], TT), ALU.mult))
                    link(nc.vector.tensor_tensor(u_sb[:], u_sb[:], bcast_rows(lnb_sb[:], TT), ALU.add))
                    link(nc.vector.tensor_tensor(u_sb[:], u_sb[:], x_sb[:], ALU.add))
                    norm(link, dve, 1, lambda t: u_sb[:, t, :], lambda t: x1_sb[:, t, :], False)
                    nc.vector.engine_nop().then_inc(S["s_x1"], 1)
                    for n in range(NK + DC):
                        parts, m, c0, w = parts_of(n)
                        dve.wait_ge(S["s_p1"], n + 1)
                        if n >= 2:
                            dve.wait_ge(S["s_p3"], n - 1)
                        nc.vector.tensor_tensor(rest[:, n % 2, 0:w], ps[:, proj_bank(n), 0:w],
                                                parts[:, 0, m, c0:c0 + w], ALU.subtract).then_inc(S["s_rest"], 1)

            with nc.Block(no_gpsimd_drain=True) as block:
                @block.sync
                def _(sp):
                    for g in range(2, NG):
                        sp.wait_ge(S["s_st"], GH * KT * (g - 1))
                        sp.wait_ge(S["s_sB"], GH * TT * (g - 1))
                        load_k(sp, g)

                @block.tensor
                def _(pe):
                    def max_tile(n):
                        g, t, j = n // (TT * GH), n // GH % TT, n % GH
                        h = g * GH + j
                        if n % (TT * GH) == 0:
                            pe.wait_ge(s_kl[g % 2], 16 * len(TERMS) * (g // 2 + 1))
                            if g:
                                pe.wait_ge(S["s_mr"], g)
                        for part, (s_scores, s_taken) in enumerate(((S["s_sA"], S["s_mA"]), (S["s_sB"], S["s_mB"]))):
                            if n:
                                pe.wait_ge(s_taken, n)
                            for c in (2 * part, 2 * part + 1):
                                c0, w = CHUNKS[c]
                                last = nc.tensor.matmul(ps[:, c, 0:w], q_aug[0:ROWS, h, t * P:(t + 1) * P],
                                                        k_aug[0:ROWS, g % 2, j, c0:c0 + w], start=True, stop=True)
                            last.then_inc(s_scores, 1)

                    def max_rows(g):
                        pe.wait_ge(S["s_mp"], g + 1)
                        rows = ps[:, 2:4, :].rearrange("p a b -> p (a b)").bitcast(BF16)
                        for j in range(GH):
                            for t in range(TT):
                                c0 = j * T + t * P
                                last = nc.tensor.transpose(rows[ROWS:ROWS + MROWS, c0:c0 + P], m_parts[:, t, j, :], ident_bf[:])
                        last.then_inc(S["s_mT"], 1)

                    def score_tile(n):
                        g, k, j = n // (KT * GH), n // GH % KT, n % GH
                        if n % (KT * GH) == 0:
                            pe.wait_ge(S["s_mr"], g + 1)
                        if n >= 3:
                            pe.wait_ge(S["s_exp"], n - 2)
                        bk, w = 4 + n % 3, KW[k]
                        for t in range(TT):
                            nc.tensor.matmul(ps[0:w, bk, t * P:(t + 1) * P], bias[:, t, k * P:k * P + w], ident_bf[:],
                                             start=(t == 0), stop=False, skip_group_check=True)
                        last = nc.tensor.matmul(ps[0:w, bk, :], k_aug[:, g % 2, j, k * P:k * P + w], q_aug[:, g * GH + j, :],
                                                start=False, stop=True, skip_group_check=True)
                        last.then_inc(S["s_st"], 1)

                    def weigh(g, k):
                        pe.wait_ge(S["s_exp"], (g * KT + k + 1) * GH)
                        if k == 0 and g:
                            pe.wait_ge(S["s_oTs"], g)
                        for j in range(GH):
                            n = (g * KT + k) * GH + j
                            last = nc.tensor.matmul(ps[32 * j:32 * j + 32, 7, :], v_aug[0:KW[k], k, g * GH + j, :],
                                                    probs[0:KW[k], n % PRING, :], start=(k == 0), stop=(k == KT - 1))
                        last.then_inc(S["s_pv"], 1)

                    pe.wait_ge(S["s_ql"], 16 * len(TERMS))
                    for n in range(TT * GH):
                        max_tile(n)
                    max_rows(0)
                    done = 0
                    for g in range(NG):
                        tiles = list(range((g + 1) * TT * GH, (g + 2) * TT * GH)) if g + 1 < NG else []
                        for k in range(KT):
                            upto = min((g * KT + k + 1) * GH + 3, (g + 1) * KT * GH)
                            while done < upto:
                                score_tile(done)
                                done += 1
                            weigh(g, k)
                            want = len(tiles) * (k + 1) // KT - len(tiles) * k // KT
                            for n in range(len(tiles) * k // KT, len(tiles) * k // KT + want):
                                max_tile(tiles[n])
                        if g + 1 < NG:
                            max_rows(g + 1)

                @block.scalar
                def _(act):
                    def rows(g):
                        act.wait_ge(S["s_mT"], g + 1)
                        src = ps[:, 2:4, :].rearrange("p a b -> p (a b)").bitcast(BF16)
                        nc.scalar.copy(q_aug[ROWS:ROWS + MROWS, g * GH:(g + 1) * GH, :].rearrange("p a b -> p (a b)"),
                                       src[ROWS:ROWS + MROWS, :]).then_inc(S["s_mr"], 1)

                    rows(0)
                    for g in range(NG):
                        for k in range(KT):
                            for j in range(GH):
                                n = (g * KT + k) * GH + j
                                act.wait_ge(S["s_st"], n + 1)
                                if n >= PRING and n % GH == 0:
                                    act.wait_ge(S["s_pv"], (n - PRING) // GH + 1)
                                nc.scalar.activation(probs[0:KW[k], n % PRING, :], ps[0:KW[k], 4 + n % 3, :], ACT.Exp,
                                                     scale=HD ** -0.5).then_inc(S["s_exp"], 1)
                        act.wait_ge(S["s_pv"], (g + 1) * KT)
                        nc.scalar.copy(oT_sb[:, g, :], bank(7)).then_inc(S["s_oTs"], 1)
                        if g + 1 < NG:
                            rows(g + 1)

                @block.vector
                def _(dve):
                    link = Link(dve)
                    base = DVE_PREPARE
                    link.n = base
                    for g in range(NG):
                        for t in range(TT):
                            for j in range(GH):
                                n = (g * TT + t) * GH + j
                                for part, (c0, c1) in enumerate(((0, HALF), (HALF, S2))):
                                    s_scores, s_taken = ((S["s_sA"], S["s_mA"]), (S["s_sB"], S["s_mB"]))[part]
                                    if n:
                                        dve.wait_ge(s_taken, n)
                                    dve.wait_ge(s_scores, n + 1)
                                    scores = ps[:, 2 * part:2 * part + 2, :].rearrange("p a b -> p (a b)")[:, 0:c1 - c0]
                                    nc.vector.tensor_tensor_reduce(
                                        out=junk[:, c0:c1], in0=scores, in1=bias[:, t, c0:c1], scale=1.0, scalar=LOWEST,
                                        op0=ALU.add, op1=ALU.max, accum_out=mx[:, part, t, j:j + 1]).then_inc(s_taken, 1)
                        dve.wait_ge(S["s_mA"], (g + 1) * TT * GH)
                        dve.wait_ge(S["s_mB"], (g + 1) * TT * GH)
                        link(nc.vector.tensor_tensor(m_full[:], mx[:, 0, :, :], mx[:, 1, :, :], ALU.max))
                        link(nc.vector.tensor_scalar(m_parts[:, :, :, 0], m_full[:], -1.0, None, ALU.mult))
                        link(nc.vector.scalar_tensor_tensor(out=m_rest[:], in0=m_full[:], scalar=-1.0, in1=m_parts[:, :, :, 0],
                                                            op0=ALU.mult, op1=ALU.subtract))
                        link(nc.vector.tensor_copy(m_parts[:, :, :, 1], m_rest[:]))
                        nc.vector.tensor_tensor(m_parts[:, :, :, 2], m_rest[:], m_parts[:, :, :, 1],
                                                ALU.subtract).then_inc(S["s_mp"], 1)
                        dve.wait_ge(S["s_mp"], g + 1)

            with nc.Block(no_gpsimd_drain=True) as block:
                @block.tensor
                def _(pe):
                    for t in range(TT):
                        for g in range(NG):
                            last = nc.tensor.transpose(ps[:, t, g * P:(g + 1) * P], oT_sb[:, g, t * P:(t + 1) * P], ident[:])
                        last.then_inc(S["s_tr"], 1)
                    for t in range(TT):
                        pe.wait_ge(S["s_on"], t + 1)
                        for c in range(DC):
                            last = nc.tensor.transpose(ps[:, 4 + t, c * P:(c + 1) * P], on_sb[:, t, c * P:(c + 1) * P], ident[:])
                        last.then_inc(S["s_tr2"], 1)
                    for t in range(TT):
                        pe.wait_ge(S["s_onT"], t + 1)
                        for c in range(DC):
                            last = nc.tensor.matmul(ps[:, t, 0:D], onT_sb[:, c, t * P:(t + 1) * P], wo_sb[:, c, :],
                                                    start=(c == 0), stop=(c == DC - 1))
                        last.then_inc(S["s_y"], 1)

                @block.scalar
                def _(act):
                    for t in range(TT):
                        act.wait_ge(S["s_tr2"], t + 1)
                        nc.scalar.copy(onT_sb[:, :, t * P:(t + 1) * P],
                                       ps[:, 4 + t, 0:D].rearrange("p (c q) -> p c q", c=DC)).then_inc(S["s_onT"], 1)

                @block.gpsimd
                def _(pool):
                    pool.wait_ge(S["s_var"], 3)
                    nc.gpsimd.tensor_tensor(rstd[:], ve[:], power[:], ALU.pow).then_inc(S["s_rstd"], 1)

                @block.vector
                def _(dve):
                    link = Link(dve)
                    link.n = DVE_PREPARE + DVE_ATTEND
                    for t in range(TT):
                        dve.wait_ge(S["s_tr"], t + 1)
                        heads = ps[:, t, :].rearrange("p (h d) -> p h d", h=H)
                        link(nc.vector.reciprocal(rsum[:, t, :], heads[:, :, HD]))
                        nc.vector.tensor_tensor(on_sb[:, t, :].rearrange("p (h d) -> p h d", h=H), heads[:, :, 0:HD],
                                                rsum[:, t, :].rearrange("p (h a) -> p h a", a=1).to_broadcast([P, H, HD]),
                                                ALU.mult).then_inc(S["s_on"], 1)
                    for t in range(TT):
                        dve.wait_ge(S["s_y"], t + 1)
                        link(nc.vector.tensor_tensor(u_sb[:, t, :], ps[:, t, 0:D], bo_sb[:], ALU.add))
                    link(nc.vector.tensor_tensor(u_sb[:], u_sb[:], x1_sb[:], ALU.add))
                    norm(link, dve, 2, lambda t: u_sb[:, t, :], lambda t: x2[:, bass.ds(b * TT + t, 1), :].rearrange("p a d -> p (a d)"), False)

            nc.all_engine_barrier(sems_to_clear=as_range(per_batch.values()))


DVE_NORM = 3 * TT
DVE_PREPARE = 2 * DVE_NORM + 3
DVE_ATTEND = 4 * NG


def mixture(nc, x2, ident, ps, router_wT, correction, up_w, down_w, out):
    with ExitStack() as ctx:
        def sb(name, shape, dt=F32):
            return ctx.enter_context(nc.sbuf_tensor(name, shape, dt))

        x2T = sb("x2T", [P, DC, NT * P])
        router_sb = sb("router_sb", [P, DC, E])
        corr_sb = sb("corr_sb", [P, E])
        lower = sb("lower", [P, G, G])
        power = sb("power_m", [P, NT])
        scores = sb("scores", [P, NT, E])
        sfc = sb("sfc", [P, NT, E])
        work = sb("work", [P, NT, E])
        work2 = sb("work2", [P, NT, E])
        m1 = sb("m1", [P, NT * G])
        m2 = sb("m2", [P, NT * G])
        cnt = sb("cnt", [P, NT * G])
        top8 = sb("top8", [P, NT, K_TOP])
        total = sb("total", [P, NT])
        combine = sb("combine", [P, NT, EXPERTS])
        wu = sb("wu", [P, 2, DC, I_MOE])
        wd = sb("wd", [P, 2, D])
        hr = sb("hr", [P, 4, 512])
        h2 = sb("h2", [P, 2, NT * P])
        stats = sb("stats_m", [P, NT, 6])
        mv = sb("mv_m", [P, NT, 2])
        ve = sb("ve_m", [P, NT])
        rstd = sb("rstd_m", [P, NT])

        S = semaphores(ctx, nc, "r_load r_const0 r_const r_xT r_xTs r_logit r_exp r_dve "
                                "s_wu0 s_wu1 s_wd0 s_wd1 s_up s_relu s_h2 "
                                "s_y2 s_y_free s_var2 s_rstd2 s_final s_store")

        with nc.Block(no_gpsimd_drain=True) as block:
            @block.sync
            def _(sp):
                sp.dma_start(router_sb[:], router_wT.rearrange("(c p) n -> p c n", p=P)).then_inc(S["r_load"], 16)
                sp.dma_start(corr_sb[:], correction.rearrange("(a n) -> a n", a=1).to_broadcast([P, E])).then_inc(S["r_load"], 16)

            @block.gpsimd
            def _(pool):
                nc.gpsimd.memset(lower[:], 1.0).then_inc(S["r_const0"], 1)
                nc.gpsimd.memset(power[:], -0.5).then_inc(S["r_const0"], 1)
                nc.gpsimd.memset(combine[:], 1.0).then_inc(S["r_const0"], 1)
                pool.wait_ge(S["r_const0"], 3)
                nc.gpsimd.affine_select(out=lower[:], in_=lower[:], compare_op=ALU.is_gt, fill=0.0,
                                        base=0, pattern=[[1, G], [-1, G]], channel_multiplier=0).then_inc(S["r_const"], 1)

            @block.tensor
            def _(pe):
                for t in range(NT):
                    if t >= 4:
                        pe.wait_ge(S["r_xTs"], t - 3)
                    for c in range(DC):
                        last = nc.tensor.transpose(ps[:, 4 + t % 4, c * P:(c + 1) * P], x2[:, t, c * P:(c + 1) * P], ident[:])
                    last.then_inc(S["r_xT"], 1)
                pe.wait_ge(S["r_load"], 32)
                for t in range(NT):
                    pe.wait_ge(S["r_xTs"], t + 1)
                    for c in range(DC):
                        last = nc.tensor.matmul(ps[:, t // 8, (t % 8) * E:(t % 8 + 1) * E], x2T[:, c, t * P:(t + 1) * P],
                                                router_sb[:, c, :], start=(c == 0), stop=(c == DC - 1))
                last.then_inc(S["r_logit"], 1)

            @block.scalar
            def _(act):
                for t in range(NT):
                    act.wait_ge(S["r_xT"], t + 1)
                    nc.scalar.copy(x2T[:, :, t * P:(t + 1) * P],
                                   ps[:, 4 + t % 4, 0:D].rearrange("p (c q) -> p c q", c=DC)).then_inc(S["r_xTs"], 1)
                act.wait_ge(S["r_logit"], 1)
                nc.scalar.activation(work[:].rearrange("p t e -> p (t e)"), ps[:, 0:2, :].rearrange("p a b -> p (a b)"),
                                     ACT.Exp, scale=-1.0).then_inc(S["r_exp"], 1)

            @block.vector
            def _(dve):
                n = [0]

                def link(ins):
                    n[0] += 1
                    ins.then_inc(S["r_dve"], 1)
                    dve.wait_ge(S["r_dve"], n[0])

                def by_group(ap):
                    return ap[:].rearrange("p t (g e) -> p (t g) e", g=G)

                def over(ap, k):
                    return ap.rearrange("p (n a) -> p n a", a=1).to_broadcast([P, ap.shape[1], k])

                dve.wait_ge(S["r_exp"], 1)
                dve.wait_ge(S["r_load"], 32)
                link(nc.vector.tensor_scalar(work[:], work[:], 1.0, None, ALU.add))
                link(nc.vector.reciprocal(scores[:], work[:]))
                link(nc.vector.tensor_tensor(sfc[:], scores[:], corr_sb[:].rearrange("p (a e) -> p a e", a=1).to_broadcast([P, NT, E]), ALU.add))
                link(nc.vector.tensor_reduce(m1[:], by_group(sfc), AX.X, ALU.max))
                link(nc.vector.tensor_tensor(by_group(work), by_group(sfc), over(m1[:], E // G), ALU.is_equal))
                link(nc.vector.tensor_reduce(cnt[:], by_group(work), AX.X, ALU.add))
                link(nc.vector.scalar_tensor_tensor(out=work2[:], in0=work[:], scalar=LOWEST, in1=sfc[:], op0=ALU.mult, op1=ALU.add))
                link(nc.vector.tensor_reduce(m2[:], by_group(work2), AX.X, ALU.max))
                link(nc.vector.tensor_scalar(cnt[:], cnt[:], 1.5, 1.0, ALU.is_gt, ALU.subtract))
                link(nc.vector.scalar_tensor_tensor(out=cnt[:], in0=cnt[:], scalar=-LOWEST, in1=m1[:], op0=ALU.mult, op1=ALU.add))
                link(nc.vector.tensor_tensor(m2[:], m2[:], cnt[:], ALU.max))
                link(nc.vector.tensor_tensor(m1[:], m1[:], m2[:], ALU.add))
                others = m1[:].rearrange("p (t a g) -> p t a g", a=1, g=G).to_broadcast([P, NT, G, G])
                itself = m1[:].rearrange("p (t g a) -> p t g a", a=1, g=G).to_broadcast([P, NT, G, G])
                w4 = work[:].rearrange("p t (g e) -> p t g e", g=G)
                v4 = work2[:].rearrange("p t (g e) -> p t g e", g=G)
                dve.wait_ge(S["r_const"], 1)
                link(nc.vector.tensor_tensor(w4, others, itself, ALU.is_gt))
                link(nc.vector.tensor_tensor(v4, others, itself, ALU.is_equal))
                link(nc.vector.tensor_tensor(v4, v4, lower[:].rearrange("p (a g) e -> p a g e", a=1).to_broadcast([P, NT, G, G]), ALU.mult))
                link(nc.vector.tensor_tensor(work[:], work[:], work2[:], ALU.add))
                link(nc.vector.tensor_reduce(cnt[:], by_group(work), AX.X, ALU.add))
                link(nc.vector.tensor_scalar(cnt[:], cnt[:], TOPK_GROUP - 0.5, None, ALU.is_lt))
                link(nc.vector.tensor_tensor(by_group(work), by_group(sfc), over(cnt[:], E // G), ALU.mult))
                for t in range(NT):
                    link(nc.vector.max(top8[:, t, :], work[:, t, :]))
                    link(nc.vector.match_replace(work2[:, t, :], top8[:, t, :], work[:, t, :], LOWEST))
                link(nc.vector.tensor_scalar(work2[:], work2[:], LOWEST / 2, None, ALU.is_lt))
                link(nc.vector.tensor_tensor(work2[:], work2[:], scores[:], ALU.mult))
                link(nc.vector.tensor_reduce(total[:], work2[:], AX.X, ALU.add))
                link(nc.vector.tensor_scalar(total[:], total[:], 1e-20, None, ALU.add))
                link(nc.vector.reciprocal(total[:], total[:]))
                link(nc.vector.tensor_tensor(work2[:], work2[:], over(total[:], E), ALU.mult))
                link(nc.vector.tensor_scalar(combine[:, :, 0:E], work2[:], ROUTE_SCALE, None, ALU.mult))

        PAIRS = NT // 2
        up_v = up_w.rearrange("e (c p) i -> p e c i", p=P)
        down_v = down_w.rearrange("e i d -> i e d")
        s_wu, s_wd = [S["s_wu0"], S["s_wu1"]], [S["s_wd0"], S["s_wd1"]]
        LOOPS = EXPERTS // 2

        def result(q):
            return h2[:].rearrange("p a b -> p (a b)")[:, q * 4 * D:(q + 1) * 4 * D].rearrange("p (t d) -> p t d", d=D)


        with nc.Block(no_gpsimd_drain=True) as block:
            @block.sync
            def _(sp):
                for s in range(2):
                    sp.dma_start(wu[:, s:s + 1, :, :], up_v[:, s:s + 1, :, :]).then_inc(s_wu[s], 16)
                    sp.dma_start(wd[:, s:s + 1, :], down_v[:, s:s + 1, :]).then_inc(s_wd[s], 16)
                with sp.Fori(1, LOOPS) as i:
                    for s in range(2):
                        sp.wait_ge(S["s_up"], i * 8 + (4 * s - 4))
                        sp.dma_start(wu[:, s:s + 1, :, :], up_v[:, bass.ds(i * 2 + s, 1), :, :]).then_inc(s_wu[s], 16)
                        sp.wait_ge(S["s_y2"], i * (2 * PAIRS) + (s - 1) * PAIRS)
                        sp.dma_start(wd[:, s:s + 1, :], down_v[:, bass.ds(i * 2 + s, 1), :]).then_inc(s_wd[s], 16)
                out_v = out.rearrange("(t p) d -> p t d", p=P)
                for q in range(4):
                    sp.wait_ge(S["s_final"], 4 * q + 4)
                    sp.dma_start(out_v[:, 4 * q:4 * q + 4, :], result(q)).then_inc(S["s_store"], 16)
                sp.wait_ge(S["s_store"], 64)

            @block.tensor
            def _(pe):
                def up(k, s, load, first=False):
                    pe.wait_ge(s_wu[s], load * 16)
                    for q in range(4):
                        if not first:
                            pe.wait_ge(S["s_relu"], k * 4 + (q - 3))
                        for c in range(DC):
                            last = nc.tensor.matmul(ps[:, q, :], wu[:, s, c, :], x2T[:, c, q * 512:(q + 1) * 512],
                                                    start=(c == 0), stop=(c == DC - 1))
                        last.then_inc(S["s_up"], 1)

                def down(k, s, load):
                    pe.wait_ge(s_wd[s], load * 16)
                    for r in range(PAIRS):
                        if r % 2 == 0:
                            pe.wait_ge(S["s_h2"], k * 4 + r // 2 + 1)
                        pe.wait_ge(S["s_y_free"], k * PAIRS + r + 1)
                        for u in range(2):
                            t = 2 * r + u
                            last = nc.tensor.matmul(ps[:, 4 + r % 4, u * D:(u + 1) * D], h2[:, s, t * P:(t + 1) * P],
                                                    wd[:, s, :], start=True, stop=True)
                        last.then_inc(S["s_y2"], 1)

                up(0, 0, 1, first=True)
                with pe.Fori(0, LOOPS - 1) as i:
                    up(i * 2 + 1, 1, i + 1)
                    down(i * 2, 0, i + 1)
                    up(i * 2 + 2, 0, i + 2)
                    down(i * 2 + 1, 1, i + 1)
                up(EXPERTS - 1, 1, LOOPS)
                down(EXPERTS - 2, 0, LOOPS)
                down(EXPERTS - 1, 1, LOOPS)

            @block.scalar
            def _(act):
                def relu(k, first=False):
                    for q in range(4):
                        if not first:
                            act.wait_ge(S["s_h2"], k * 4 + (q - 3))
                        act.wait_ge(S["s_up"], k * 4 + (q + 1))
                        nc.scalar.activation(hr[:, q, :], ps[:, q, :], ACT.Relu).then_inc(S["s_relu"], 1)

                relu(0, first=True)
                with act.Fori(1, EXPERTS) as k:
                    relu(k)

            @block.gpsimd
            def _(pool):
                def square(k, s, first=False):
                    if not first:
                        pool.wait_ge(S["s_y2"], k * PAIRS - PAIRS)
                    for q in range(4):
                        pool.wait_ge(S["s_relu"], k * 4 + (q + 1))
                        nc.gpsimd.tensor_tensor(h2[:, s, q * 512:(q + 1) * 512], hr[:, q, :], hr[:, q, :],
                                                ALU.mult).then_inc(S["s_h2"], 1)

                square(0, 0, first=True)
                square(1, 1, first=True)
                with pool.Fori(1, LOOPS) as i:
                    square(i * 2, 0)
                    square(i * 2 + 1, 1)
                pool.wait_ge(S["s_var2"], 1)
                nc.gpsimd.tensor_tensor(rstd[:], ve[:], power[:], ALU.pow).then_inc(S["s_rstd2"], 1)

            @block.vector
            def _(dve):
                dve.sem_inc(S["s_y_free"], 4)
                with dve.Fori(0, EXPERTS) as k:
                    for r in range(PAIRS):
                        dve.wait_ge(S["s_y2"], k * PAIRS + r + 1)
                        for u in range(2):
                            t = 2 * r + u
                            last = nc.vector.scalar_tensor_tensor(
                                out=x2[:, t, :], in0=ps[:, 4 + r % 4, u * D:(u + 1) * D],
                                scalar=combine[:, t, bass.ds(k, 1)], in1=x2[:, t, :], op0=ALU.mult, op1=ALU.add)
                        last.then_inc(S["s_y_free"], 1)
                dve.wait_ge(S["s_y_free"], EXPERTS * PAIRS + 4)
                base = [DVE_ROUTE]

                def counted(ins):
                    base[0] += 1
                    ins.then_inc(S["r_dve"], 1)
                for t in range(NT):
                    counted(nc.vector.bn_stats(stats[:, t, :], x2[:, t, :]))
                dve.wait_ge(S["r_dve"], base[0])
                for t in range(NT):
                    counted(nc.vector.bn_aggr(mv[:, t, :], stats[:, t, :]))
                dve.wait_ge(S["r_dve"], base[0])
                nc.vector.tensor_scalar(ve[:], mv[:, :, 1], EPS, None, ALU.add).then_inc(S["s_var2"], 1)
                dve.wait_ge(S["s_rstd2"], 1)
                for t in range(NT):
                    nc.vector.tensor_scalar(result(t // 4)[:, t % 4, :], x2[:, t, :], mv[:, t, 0:1], rstd[:, t:t + 1],
                                            ALU.subtract, ALU.mult).then_inc(S["s_final"], 1)


DVE_ROUTE = 19 + 2 * NT + 7


def kernel(x, ctx_1024, mask_Bx1xSxS2_if1, L0_attn_W_qkv, L0_attn_b_qkv, L0_attn_ln_w, L0_attn_ln_b,
           L0_xattn_Wq, L0_xattn_Wk, L0_xattn_Wv, L0_xattn_Wo, L0_xattn_bo, L0_ffn_router_w,
           L0_ffn_correction_bias, L0_ffn_up_w, L0_ffn_down_w, L0_ffn_shared_up_w, L0_ffn_shared_down_w):
    import numpy as np
    import concourse.bacc as bacc
    from concourse.bass_utils import run_bass_kernel_spmd

    x_rows = np.asarray(x).reshape(B * T, D)
    shared_up = np.asarray(L0_ffn_shared_up_w).reshape(D, EXPERTS - E, I_MOE).transpose(1, 0, 2)
    shared_down = np.asarray(L0_ffn_shared_down_w).reshape(EXPERTS - E, I_MOE, D)
    given = {
        "x": x_rows, "xT": x_rows.T,
        "ctxT": np.asarray(ctx_1024).transpose(0, 2, 1).reshape(B * D, S2),
        "mask": np.asarray(mask_Bx1xSxS2_if1).reshape(B * T, S2),
        "w_qkv": L0_attn_W_qkv, "b_qkv": L0_attn_b_qkv, "ln_w": L0_attn_ln_w, "ln_b": L0_attn_ln_b,
        "wqT": np.asarray(L0_xattn_Wq).T, "wkT": np.asarray(L0_xattn_Wk).T,
        "wvT": np.asarray(L0_xattn_Wv).T, "woT": np.asarray(L0_xattn_Wo).T, "bo": L0_xattn_bo,
        "router_wT": np.asarray(L0_ffn_router_w).T, "correction": L0_ffn_correction_bias,
        "up_w": np.concatenate([np.asarray(L0_ffn_up_w), shared_up]),
        "down_w": np.concatenate([np.asarray(L0_ffn_down_w), shared_down]),
    }
    nc = bacc.Bacc("TRN2", target_bir_lowering=False, num_devices=1)
    arrays, args = {}, []
    for name, a in given.items():
        a = np.ascontiguousarray(a)
        arrays[f"in_{name}"] = a
        args.append(nc.dram_tensor(f"in_{name}", a.shape, mybir.dt.from_np(a.dtype), kind="ExternalInput").ap())
    args.append(nc.dram_tensor("out_dram", (B * T, D), F32, kind="ExternalOutput").ap())
    decoder_layer(nc, *args)
    r = run_bass_kernel_spmd(nc, [arrays], core_ids=[0])
    return r.results[0]["out_dram"].reshape(B, T, D)
```

```python
import concourse.bass as bass
from concourse import mybir
from contextlib import ExitStack

F32, BF16, I32 = mybir.dt.float32, mybir.dt.bfloat16, mybir.dt.int32
F32R = mybir.dt.float32r
ALU, ACT, AX = mybir.AluOpType, mybir.ActivationFunctionType, mybir.AxisListType

P = 128
B, T, D = 4, 512, 256
S2 = 1601
H, HD = 16, 16
SPAN = 64
E, I_MOE, I_SHARED = 64, 128, 512
EXPERTS = E + I_SHARED // I_MOE
G, TOPK_GROUP, K_TOP = 8, 4, 8
ROUTE_SCALE = 2.5
EPS = 1e-5
MASKED = -1e20
LOWEST = -1e30

DC = D // P
TT = T // P
NT = B * TT
KT = -(-S2 // P)
KW = [min(P, S2 - P * k) for k in range(KT)]
CHUNKS = [(c, min(512, S2 - c)) for c in range(0, S2, 512)]
GH = 4
NG = H // GH
TERMS = [(0, 0), (0, 1), (0, 2), (1, 0), (1, 1), (2, 0)]
ROWS = len(TERMS) * HD
MROWS = 3
K_ROWS = [(0, 3, 0), (3, 2, 0), (5, 1, 0)]
Q_ROWS = [(0, 3, 0), (3, 2, 1), (5, 1, 2)]
PASSES = [(a, w, c) for a, w in ((0, 0), (0, 1), (1, 0)) for c in range(DC)]
MAX_CHUNKS = [(c, min(401, S2 - c)) for c in range(0, S2, 401)]
GROUP_CHUNKS = len(MAX_CHUNKS) * TT * GH
WEIGH_LAG = 2
PRING = 8
SRING = 3
OUT_BANK = 7

PROJ = [(False, 0, c, w) for c, w in CHUNKS] + [(True, m, 0, T) for m in range(DC)] + [(False, 1, c, w) for c, w in CHUNKS]
PIECES = len(PROJ)
STEPS = ([("qk", m) for m in range(2 * DC)] + [("v", 0), ("v", 1), ("band", 0), ("band", 1), ("o", 0), ("o", 1)]
         + [("piece", i, *PROJ[i]) for i in range(4)] + [("x1T", 0), ("x1T", 1)]
         + [("piece", i, *PROJ[i]) for i in range(4, PIECES)]
         + [("vx", i) for i in range(-(-KT // 2))] + [("any", 0)])
PIECE_STEPS = [n for n, step in enumerate(STEPS) if step[0] == "piece"]
STEP_BANKS = [2, 3]
FIRST_BANKS = [2, 3, 4, 5, 6, 7]
EARLY = PIECE_STEPS[-1] + 1
STEPS_AT = {}
for _n in range(len(STEPS)):
    STEPS_AT.setdefault(1 + _n * 8 // 5 if _n < EARLY else 36 + 2 * (_n - EARLY), []).append(_n)
NORM_PARTS = 7
NORMS_AT = 1 + 9 * 8 // 5 + 2
MAX_SPAN = [(0, 11), (2, 11), (2, 11), (3, 13)]


def semaphores(ctx, nc, names):
    return {n: ctx.enter_context(nc.semaphore(n)) for n in names.split()}


def as_range(sems):
    numbers = sorted(s.num for s in sems)
    assert numbers == list(range(numbers[0], numbers[0] + len(numbers)))
    return range(numbers[0], numbers[-1] + 1)


def decoder_layer(nc, x, xT, ctxT, mask, w_qkv, b_qkv, ln_w, ln_b, wqT, wkT, wvT, woT, bo,
                  router_wT, correction, up_w, down_w, out):
    k_dram = nc.dram_tensor("k_dram", (B, ROWS, H, S2), BF16).ap()
    q_dram = nc.dram_tensor("q_dram", (B, ROWS, H, T), BF16).ap()
    x2_dram = nc.dram_tensor("x2_dram", (B * T, D), F32).ap()

    with ExitStack() as ctx:
        ident = ctx.enter_context(nc.sbuf_tensor("ident", [P, P], F32))
        ident_bf = ctx.enter_context(nc.sbuf_tensor("ident_bf", [P, P], BF16))
        ps = ctx.enter_context(nc.psum_tensor("ps", [P, 8, 512], F32))

        attention(nc, ident, ident_bf, ps, k_dram, q_dram, x2_dram, x, xT, ctxT, mask,
                  w_qkv, b_qkv, ln_w, ln_b, wqT, wkT, wvT, woT, bo)
        mixture(nc, x2_dram, ident, ps, router_wT, correction, up_w, down_w, out)


def attention(nc, ident, ident_bf, ps, k_dram, q_dram, x2_dram, x, xT, ctxT, mask,
              w_qkv, b_qkv, ln_w, ln_b, wqT, wkT, wvT, woT, bo):
    with ExitStack() as ctx:
        def sb(name, shape, dt=F32):
            return ctx.enter_context(nc.sbuf_tensor(name, shape, dt))

        band = sb("band", [P, 2 * P])
        w_qkv_sb = sb("w_qkv_sb", [P, DC, 3 * D])
        wq_sb = sb("wq_sb", [P, DC, D])
        wk_sb = sb("wk_sb", [P, DC, D])
        wv_sb = sb("wv_sb", [P, DC, D])
        wo_sb = sb("wo_sb", [P, DC, D])
        qk_bias = sb("qk_bias", [P, 2 * DC])
        v_bias = sb("v_bias", [P, D])
        lnw_sb = sb("lnw_sb", [P, D])
        lnb_sb = sb("lnb_sb", [P, D])
        bo_sb = sb("bo_sb", [P, D])
        power = sb("power", [P, TT])
        ones_bf = sb("ones_bf", [P, 1], BF16)

        k_aug = sb("k_aug", [ROWS + MROWS, 2, GH, S2], BF16)
        q_aug = sb("q_aug", [ROWS + MROWS, 2, GH, T], BF16)
        v_aug = sb("v_aug", [P, KT, H, HD + 1])
        bias = sb("bias", [P, TT, S2], BF16)
        probs = sb("probs", [P, PRING, T])
        oT_sb = sb("oT_sb", [P, NG, T])
        x1_sb = sb("x1_sb", [P, TT, D])
        any_masked = sb("any_masked", [1, 1], I32)

        bias_next = sb("bias_next", [P, TT, S2], BF16)
        v_next = sb("v_next", [P, KT, D])
        x1_next = sb("x1_next", [P, TT, D])
        ctx_sb = sb("ctx_sb", [P, DC, S2])
        mask_sb = sb("mask_sb", [P, S2], I32)
        xT_sb = sb("xT_sb", [P, DC, T])
        x1T_sb = xT_sb
        x_sb = sb("x_sb", [P, TT, D])
        u_sb = sb("u_sb", [P, TT, D])
        qk_sb = sb("qk_sb", [P, 2 * DC, T])
        v_sb = sb("v_sb", [P, TT, D])
        st_sb = sb("st_sb", [P, TT, 2 * P])
        parts = sb("parts", [P, 3, SRING, 512], BF16)
        rest = sb("rest", [P, 2, 512])
        on_sb = v_sb
        onT_sb = st_sb[:].rearrange("p t d -> p (t d)").rearrange("p (c q) -> p c q", c=DC)
        x2_sb = qk_sb[:, 0:2, :].rearrange("p a b -> p (a b)").rearrange("p (t d) -> p t d", t=TT)

        stats = sb("stats", [P, TT, 6])
        mv = sb("mv", [P, TT, 2])
        ve = sb("ve", [P, TT])
        rstd = sb("rstd", [P, TT])
        mx = sb("mx", [P, 4, TT * GH])
        m_two = sb("m_two", [P, 2, TT * GH])
        m_full = sb("m_full", [P, TT * GH])
        m_rest = sb("m_rest", [P, TT * GH])
        m_parts = sb("m_parts", [P, TT * GH, MROWS], BF16)
        rsum = sb("rsum", [P, TT, H])
        lowest_sum = sb("lowest_sum", [1, 1])

        once = semaphores(ctx, nc, "s_weights s_ident0 s_ident s_const s_ones")
        s_weights, s_ident0, s_ident, s_const, s_ones = once.values()

        with nc.Block(no_gpsimd_drain=True) as block:
            @block.sync
            def _(sp):
                for dst, src in ((w_qkv_sb, w_qkv), (wq_sb, wqT), (wk_sb, wkT), (wv_sb, wvT), (wo_sb, woT)):
                    sp.dma_start(dst[:], src.rearrange("(c p) n -> p c n", p=P)).then_inc(s_weights, 16)
                with nc.allow_non_contiguous_dma(reason="512 bias values, once"):
                    sp.dma_start(qk_bias[:], b_qkv[0:2 * D].rearrange("(c p) -> p c", p=P)).then_inc(s_weights, 16)
                for dst, src in ((v_bias, b_qkv[2 * D:3 * D]), (lnw_sb, ln_w), (lnb_sb, ln_b), (bo_sb, bo)):
                    sp.dma_start(dst[:], src.rearrange("(a n) -> a n", a=1).to_broadcast([P, D])).then_inc(s_weights, 16)
                sp.wait_ge(s_weights, 16 * 10)

            @block.gpsimd
            def _(pool):
                nc.gpsimd.memset(ident[:], 0.0).then_inc(s_ident0, 1)
                nc.gpsimd.memset(band[:], 1.0 / (D * SPAN) ** 0.5).then_inc(s_ident0, 1)
                nc.gpsimd.memset(power[:], -0.5).then_inc(s_ident0, 1)
                pool.wait_ge(s_ident0, 2)
                nc.gpsimd.affine_select(out=ident[:], in_=ident[:], compare_op=ALU.not_equal, fill=1.0,
                                        base=0, pattern=[[-1, P]], channel_multiplier=1).then_inc(s_ident, 1)
                nc.gpsimd.affine_select(out=band[:], in_=band[:], compare_op=ALU.is_ge, fill=0.0,
                                        base=0, pattern=[[1, 2 * P]], channel_multiplier=-1).then_inc(s_const, 1)
                pool.wait_ge(s_const, 1)
                nc.gpsimd.affine_select(out=band[:], in_=band[:], compare_op=ALU.is_ge, fill=0.0,
                                        base=SPAN - 1, pattern=[[-1, 2 * P]], channel_multiplier=1).then_inc(s_const, 1)
                pool.wait_ge(s_const, 2)

            @block.vector
            def _(dve):
                nc.vector.memset(v_aug[:], 1.0).then_inc(s_ones, 1)
                nc.vector.memset(k_aug[ROWS:ROWS + MROWS, :, :, :], 1.0).then_inc(s_ones, 1)
                dve.wait_ge(s_ident, 1)
                nc.vector.tensor_copy(ident_bf[:], ident[:]).then_inc(s_ones, 1)
                nc.vector.memset(ones_bf[:], 1.0).then_inc(s_ones, 1)
                nc.vector.memset(ps[:, OUT_BANK, :], 0.0).then_inc(s_ones, 1)
                dve.wait_ge(s_ones, 5)

        per_batch = semaphores(
            ctx, nc,
            "s_x s_ctx s_mask s_bias s_step s_qk_sb s_v_sb s_band_sb s_u s_rest s_first s_second s_third "
            "s_var s_rstd s_x1 s_x1T_sb s_vx_sb s_flag s_dve s_store0 s_store1 s_store2 s_kl0 s_kl1 "
            "s_max s_max_taken s_mp s_mT s_mr s_st s_exp s_pv s_oTs "
            "s_tr s_on s_tr2 s_onT s_y s_residual s_x2 s_x2_out s_next")
        S = per_batch
        s_store = [S["s_store0"], S["s_store1"], S["s_store2"]]
        s_kl = [S["s_kl0"], S["s_kl1"]]

        class Link:
            def __init__(self, dve):
                self.dve, self.n = dve, 0

            def __call__(self, ins):
                self.n += 1
                ins.then_inc(S["s_dve"], 1)
                self.dve.wait_ge(S["s_dve"], self.n)

        def norm_stats(link, dve, src):
            for t in range(TT):
                nc.vector.bn_stats(stats[:, t, :], src[:, t, :]).then_inc(S["s_dve"], 1)
                link.n += 1
            dve.wait_ge(S["s_dve"], link.n)
            for t in range(TT):
                nc.vector.bn_aggr(mv[:, t, :], stats[:, t, :]).then_inc(S["s_dve"], 1)
                link.n += 1
            dve.wait_ge(S["s_dve"], link.n)
            nc.vector.tensor_scalar(ve[:], mv[:, :, 1], EPS, None, ALU.add).then_inc(S["s_var"], 1)

        def norm_apply(link, dve, count, src, dst):
            dve.wait_ge(S["s_rstd"], count)
            for t in range(TT):
                nc.vector.tensor_scalar(dst[:, t, :], src[:, t, :], mv[:, t, 0:1], rstd[:, t:t + 1],
                                        ALU.subtract, ALU.mult).then_inc(S["s_dve"], 1)
                link.n += 1
            dve.wait_ge(S["s_dve"], link.n)

        def rsqrt(pool, n):
            pool.wait_ge(S["s_var"], n + 1)
            nc.gpsimd.tensor_tensor(rstd[:], ve[:], power[:], ALU.pow).then_inc(S["s_rstd"], 1)

        def bcast_rows(ap, n):
            return ap.rearrange("p (a d) -> p a d", a=1).to_broadcast([P, n, ap.shape[1]])

        def taken(n):
            kind, i = STEPS[n][:2]
            return {"qk": (S["s_qk_sb"], i + 1), "v": (S["s_v_sb"], i + 1), "band": (S["s_band_sb"], 2 * i + 2),
                    "o": (S["s_u"], i + 1), "piece": (S["s_rest"], i + 1), "x1T": (S["s_x1T_sb"], i + 1),
                    "vx": (S["s_vx_sb"], i + 1)}[kind]

        def pe_step(pe, n, banks):
            kind, i = STEPS[n][:2]
            bk = banks[n % len(banks)]
            if n >= len(banks):
                pe.wait_ge(*taken(n - len(banks)))
            if kind == "qk":
                if i == 0:
                    pe.wait_ge(S["s_x"], 32)
                for c in range(DC):
                    last = nc.tensor.matmul(ps[:, bk, :], w_qkv_sb[:, c, i * P:(i + 1) * P], xT_sb[:, c, :],
                                            start=(c == 0), stop=(c == DC - 1))
            elif kind == "v":
                for u in range(2):
                    t = 2 * i + u
                    for c in range(DC):
                        last = nc.tensor.matmul(ps[:, bk, u * D:(u + 1) * D], xT_sb[:, c, t * P:(t + 1) * P],
                                                w_qkv_sb[:, c, 2 * D:3 * D], start=(c == 0), stop=(c == DC - 1))
            elif kind == "band":
                pe.wait_ge(S["s_qk_sb"], 2 * DC)
                for u in range(2):
                    t = 2 * i + u
                    w = min(2 * P, T - t * P)
                    for c in range(DC):
                        last = nc.tensor.matmul(ps[:, bk, u * 2 * P:u * 2 * P + w], qk_sb[:, DC + c, t * P:(t + 1) * P],
                                                qk_sb[:, c, t * P:t * P + w], start=(c == 0), stop=(c == DC - 1))
            elif kind == "o":
                pe.wait_ge(S["s_v_sb"], 2)
                pe.wait_ge(S["s_band_sb"], TT)
                for u in range(2):
                    t = 2 * i + u
                    last = nc.tensor.matmul(ps[:, bk, u * D:(u + 1) * D], st_sb[:, t, 0:P], v_sb[:, t, :],
                                            start=True, stop=(t == 0))
                    if t:
                        last = nc.tensor.matmul(ps[:, bk, u * D:(u + 1) * D], st_sb[:, t - 1, P:2 * P], v_sb[:, t - 1, :],
                                                start=False, stop=True)
            elif kind == "piece":
                is_q, m, c0, w = STEPS[n][2:]
                if is_q:
                    pe.wait_ge(S["s_x1T_sb"], DC)
                else:
                    pe.wait_ge(S["s_ctx"], 16)
                weight, source = (wq_sb, x1T_sb) if is_q else (wk_sb, ctx_sb)
                for c in range(DC):
                    last = nc.tensor.matmul(ps[:, bk, 0:w], weight[:, c, m * P:(m + 1) * P], source[:, c, c0:c0 + w],
                                            start=(c == 0), stop=(c == DC - 1))
            elif kind == "x1T":
                pe.wait_ge(S["s_x1"], 1)
                for t in range(TT):
                    last = nc.tensor.transpose(ps[:, bk, t * P:(t + 1) * P], x1_next[:, t, i * P:(i + 1) * P], ident[:])
            elif kind == "vx":
                for k in range(2 * i, min(2 * i + 2, KT)):
                    for c in range(DC):
                        last = nc.tensor.matmul(ps[0:KW[k], bk, k % 2 * D:(k % 2 + 1) * D], ctx_sb[:, c, k * P:k * P + KW[k]],
                                                wv_sb[:, c, :], start=(c == 0), stop=(c == DC - 1))
            else:
                pe.wait_ge(S["s_bias"], TT)
                for t in range(TT):
                    for c0, w in MAX_CHUNKS:
                        last = nc.tensor.matmul(ps[0:1, bk, 0:w], ones_bf[:], bias_next[:, t, c0:c0 + w],
                                                start=(t == 0 and c0 == 0), stop=(t == TT - 1 and c0 + w == S2),
                                                skip_group_check=True)
            last.then_inc(S["s_step"], 1)

        def act_step(act, n, banks):
            kind, i = STEPS[n][:2]
            bk = banks[n % len(banks)]
            if kind in ("v", "band", "any"):
                return
            act.wait_ge(S["s_step"], n + 1)
            if kind == "qk":
                nc.scalar.activation(qk_sb[:, i, :], ps[:, bk, :], ACT.Identity, bias=qk_bias[:, i:i + 1]).then_inc(S["s_qk_sb"], 1)
            elif kind == "o":
                nc.scalar.copy(u_sb[:, 2 * i:2 * i + 2, :].rearrange("p t d -> p (t d)"), ps[:, bk, :]).then_inc(S["s_u"], 1)
            elif kind == "piece":
                w = STEPS[n][5]
                if i >= SRING:
                    act.wait_ge(s_store[i % SRING], 16 * 3 * (i // SRING))
                nc.scalar.copy(parts[:, 0, i % SRING, 0:w], ps[:, bk, 0:w]).then_inc(S["s_first"], 1)
            elif kind == "x1T":
                nc.scalar.copy(x1T_sb[:, i, :], ps[:, bk, :]).then_inc(S["s_x1T_sb"], 1)
            elif 2 * i + 1 < KT:
                nc.scalar.copy(v_next[:, 2 * i:2 * i + 2, :].rearrange("p t d -> p (t d)"), ps[:, bk, :]).then_inc(S["s_vx_sb"], 1)
            else:
                nc.scalar.copy(v_next[0:KW[2 * i], 2 * i, :], ps[0:KW[2 * i], bk, 0:D]).then_inc(S["s_vx_sb"], 1)

        def act_second(act, n):
            i, w = STEPS[n][1], STEPS[n][5]
            act.wait_ge(S["s_rest"], i + 1)
            nc.scalar.copy(parts[:, 1, i % SRING, 0:w], rest[:, i % 2, 0:w]).then_inc(S["s_second"], 1)

        def pool_third(pool, i):
            w = STEPS[PIECE_STEPS[i]][5]
            pool.wait_ge(S["s_second"], i + 1)
            nc.gpsimd.tensor_tensor(parts[:, 2, i % SRING, 0:w], rest[:, i % 2, 0:w],
                                    parts[:, 1, i % SRING, 0:w], ALU.subtract).then_inc(S["s_third"], 1)

        def pool_mask(pool, t):
            pool.wait_ge(S["s_mask"], 16 * (t + 1))
            nc.gpsimd.tensor_scalar(bias_next[:, t, :], mask_sb[:], 0.0, MASKED,
                                    ALU.is_equal, ALU.mult).then_inc(S["s_bias"], 1)

        def dve_step(dve, link, n, banks):
            kind, i = STEPS[n][:2]
            bk = banks[n % len(banks)]
            if kind == "v":
                dve.wait_ge(S["s_step"], n + 1)
                nc.vector.tensor_tensor(v_sb[:, 2 * i:2 * i + 2, :], ps[:, bk, :].rearrange("p (t d) -> p t d", d=D),
                                        bcast_rows(v_bias[:], 2), ALU.add).then_inc(S["s_v_sb"], 1)
            elif kind == "band":
                dve.wait_ge(S["s_step"], n + 1)
                for u in range(2):
                    t = 2 * i + u
                    w = min(2 * P, T - t * P)
                    nc.vector.tensor_tensor(st_sb[:, t, 0:w], ps[:, bk, u * 2 * P:u * 2 * P + w], band[:, 0:w],
                                            ALU.mult).then_inc(S["s_band_sb"], 1)
            elif kind == "piece":
                w = STEPS[n][5]
                dve.wait_ge(S["s_first"], i + 1)
                if i >= 2:
                    dve.wait_ge(S["s_third"], i - 1)
                nc.vector.tensor_tensor(rest[:, i % 2, 0:w], ps[:, bk, 0:w], parts[:, 0, i % SRING, 0:w],
                                        ALU.subtract).then_inc(S["s_rest"], 1)
            elif kind == "any":
                dve.wait_ge(S["s_step"], n + 1)
                link(nc.vector.tensor_reduce(lowest_sum[:], ps[0:1, bk, 0:MAX_CHUNKS[0][1]], AX.X, ALU.min))
                nc.vector.tensor_scalar(any_masked[:], lowest_sum[:], 0.0, None, ALU.is_lt).then_inc(S["s_flag"], 1)

        def dve_norms(dve, link, part):
            if part == 0:
                dve.wait_ge(S["s_u"], 2)
                norm_stats(link, dve, u_sb)
            elif part == 1:
                norm_apply(link, dve, 1, u_sb, u_sb)
            elif part == 2:
                link(nc.vector.tensor_tensor(u_sb[:], u_sb[:], bcast_rows(lnw_sb[:], TT), ALU.mult))
            elif part == 3:
                link(nc.vector.tensor_tensor(u_sb[:], u_sb[:], bcast_rows(lnb_sb[:], TT), ALU.add))
            elif part == 4:
                link(nc.vector.tensor_tensor(u_sb[:], u_sb[:], x_sb[:], ALU.add))
            elif part == 5:
                norm_stats(link, dve, u_sb)
            else:
                norm_apply(link, dve, 2, u_sb, x1_next)
                nc.vector.engine_nop().then_inc(S["s_x1"], 1)

        def load_rows(sp, row, mask_row):
            sp.dma_start(xT_sb[:], xT[:, row].rearrange("(c p) t -> p c t", p=P)).then_inc(S["s_x"], 16)
            sp.dma_start(x_sb[:], x[row, :].rearrange("(t p) d -> p t d", p=P)).then_inc(S["s_x"], 16)
            load_mask(sp, mask_row, 0)

        def load_ctx(sp, row):
            sp.dma_start(ctx_sb[:], ctxT[row, :].rearrange("(c p) n -> p c n", p=P)).then_inc(S["s_ctx"], 16)

        def load_mask(sp, mask_row, t):
            if t:
                sp.wait_ge(S["s_bias"], t)
            sp.dma_start(mask_sb[:], mask[mask_row(t), :]).then_inc(S["s_mask"], 16)

        def store_piece(sp, i, batch):
            is_q, m, c0, w = STEPS[PIECE_STEPS[i]][2:]
            sp.wait_ge(S["s_third"], i + 1)
            for row, count, part in (Q_ROWS if is_q else K_ROWS):
                dst = (q_dram if is_q else k_dram)[batch].rearrange("a (i p) h n -> (a i) (p h) n", p=HD)
                src = parts[:, part:part + count, i % SRING, 0:w] if not is_q else \
                    parts[:, part:part + 1, i % SRING, 0:w].to_broadcast([P, count, w])
                sp.dma_start(dst[row:row + count, m * P:(m + 1) * P, c0:c0 + w].rearrange("i r n -> r i n"),
                             src).then_inc(s_store[i % SRING], 16)

        def stores_done(sp):
            for s in range(SRING):
                sp.wait_ge(s_store[s], 16 * 3 * len(range(s, PIECES, SRING)))

        def load_group(sp, g, slot, batch):
            for dst, src in ((k_aug, k_dram), (q_aug, q_dram)):
                sp.dma_start(dst[0:ROWS, slot, :, :], src[batch, :, g * GH:(g + 1) * GH, :].rearrange("a r h n -> (a r) h n")).then_inc(s_kl[slot], 16)

        def pe_max(pe, n, slot):
            part, j, t = n % 4, n // 4 % GH, n // 16 % TT
            if n >= 2:
                pe.wait_ge(S["s_max_taken"], n - 1)
            if n % GROUP_CHUNKS == 0 and n:
                pe.wait_ge(S["s_mr"], n // GROUP_CHUNKS)
            c0, w = MAX_CHUNKS[part]
            nc.tensor.matmul(ps[:, n % 2, 0:w], q_aug[0:ROWS, slot, j, t * P:(t + 1) * P],
                             k_aug[0:ROWS, slot, j, c0:c0 + w], start=True, stop=True).then_inc(S["s_max"], 1)

        def dve_max(dve, n, terms):
            part, j, t = n % 4, n // 4 % GH, n // 16 % TT
            c0, w = MAX_CHUNKS[part]
            dve.wait_ge(S["s_max"], n + 1)
            nc.vector.tensor_tensor_reduce(
                out=ps[:, n % 2, 0:w], in0=ps[:, n % 2, 0:w], in1=terms[:, t, c0:c0 + w], scale=1.0, scalar=LOWEST,
                op0=ALU.add, op1=ALU.max, accum_out=mx[:, part, t * GH + j:t * GH + j + 1]).then_inc(S["s_max_taken"], 1)

        def dve_max_parts(dve, link, count):
            dve.wait_ge(S["s_max_taken"], count * GROUP_CHUNKS)
            if count > 1:
                dve.wait_ge(S["s_mT"], count - 1)
            link(nc.vector.tensor_tensor(m_two[:], mx[:, 0:2, :], mx[:, 2:4, :], ALU.max))
            link(nc.vector.tensor_tensor(m_full[:], m_two[:, 0, :], m_two[:, 1, :], ALU.max))
            link(nc.vector.tensor_scalar(m_parts[:, :, 0], m_full[:], -1.0, None, ALU.mult))
            link(nc.vector.scalar_tensor_tensor(out=m_rest[:], in0=m_full[:], scalar=-1.0, in1=m_parts[:, :, 0],
                                                op0=ALU.mult, op1=ALU.subtract))
            link(nc.vector.tensor_copy(m_parts[:, :, 1], m_rest[:]))
            nc.vector.tensor_tensor(m_parts[:, :, 2], m_rest[:], m_parts[:, :, 1], ALU.subtract).then_inc(S["s_mp"], 1)
            dve.wait_ge(S["s_mp"], count)

        max_rows = ps[ROWS:ROWS + MROWS, 0:2, :].rearrange("p a b -> p (a b)").bitcast(BF16)

        def pe_max_rows(pe, count):
            pe.wait_ge(S["s_mp"], count)
            for j in range(GH):
                for t in range(TT):
                    c0 = j * T + t * P
                    last = nc.tensor.transpose(max_rows[:, c0:c0 + P], m_parts[:, t * GH + j, :], ident_bf[:])
            last.then_inc(S["s_mT"], 1)

        def act_max_rows(act, count, slot):
            act.wait_ge(S["s_mT"], count)
            nc.scalar.copy(q_aug[ROWS:ROWS + MROWS, slot, :, :].rearrange("p a b -> p (a b)"), max_rows).then_inc(S["s_mr"], 1)

        def attend(batch, row, mask_row, ctx_row, next_batch, following):
            groups_max = NG if following else NG - 1

            def chunk_range(g, k):
                first, last = MAX_SPAN[g]
                if g >= groups_max or not first <= k < last:
                    return range(0)
                a, z = (GROUP_CHUNKS * (k + d - first) // (last - first) for d in (0, 1))
                return range(g * GROUP_CHUNKS + a, g * GROUP_CHUNKS + z)

            with nc.Block(no_gpsimd_drain=True) as block:
                @block.sync
                def _(sp):
                    if following:
                        load_rows(sp, row, mask_row)
                        load_ctx(sp, ctx_row)
                        for t in range(1, TT - 1):
                            load_mask(sp, mask_row, t)

                    def group(g):
                        sp.wait_ge(S["s_st"], GH * KT * (g - 1))
                        if g > 2:
                            sp.wait_ge(S["s_max"], GROUP_CHUNKS * (g - 2))
                        load_group(sp, g % NG, g % 2, next_batch if g == NG else batch)

                    group(2)
                    if following:
                        load_mask(sp, mask_row, TT - 1)
                        for i in range(4):
                            store_piece(sp, i, next_batch)
                    group(3)
                    if following:
                        for i in range(4, PIECES):
                            store_piece(sp, i, next_batch)
                        stores_done(sp)
                        group(4)

                @block.tensor
                def _(pe):
                    def score_tile(n, masked):
                        g, k, j = n // (KT * GH), n // GH % KT, n % GH
                        if n % (KT * GH) == 0 and g:
                            pe.wait_ge(S["s_mr"], g)
                        if n >= 3:
                            pe.wait_ge(S["s_exp"], n - 2)
                        bk, w = 4 + n % 3, KW[k]
                        for t in range(TT if masked else 0):
                            nc.tensor.matmul(ps[0:w, bk, t * P:(t + 1) * P], bias[:, t, k * P:k * P + w], ident_bf[:],
                                             start=(t == 0), stop=False, skip_group_check=True)
                        last = nc.tensor.matmul(ps[0:w, bk, :], k_aug[:, g % 2, j, k * P:k * P + w], q_aug[:, g % 2, j, :],
                                                start=not masked, stop=True, skip_group_check=masked)
                        last.then_inc(S["s_st"], 1)

                    def weigh(n):
                        g, k, j = n // (KT * GH), n // GH % KT, n % GH
                        if k == 0 and j == 0 and g:
                            pe.wait_ge(S["s_oTs"], g)
                        pe.wait_ge(S["s_exp"], n + 1)
                        nc.tensor.matmul(ps[32 * j:32 * j + HD + 1, OUT_BANK, :], v_aug[0:KW[k], k, g * GH + j, :],
                                         probs[0:KW[k], n % PRING, :], start=(k == 0), stop=(k == KT - 1)).then_inc(S["s_pv"], 1)

                    def groups(masked):
                        done = 0
                        for g in range(NG):
                            for k in range(KT):
                                i = g * KT + k
                                chunks = list(chunk_range(g, k))
                                if chunks and k == MAX_SPAN[g][0] and g:
                                    pe.wait_ge(s_kl[(g + 1) % 2], 32 * (2 if g == 3 else 1))
                                for j in range(GH):
                                    upto = min(i * GH + 4 + j, NG * KT * GH)
                                    while done < upto:
                                        score_tile(done, masked)
                                        done += 1
                                    for n in chunks[len(chunks) * j // GH:len(chunks) * (j + 1) // GH]:
                                        pe_max(pe, n, (g + 1) % 2)
                                    if i * GH + j >= WEIGH_LAG:
                                        weigh(i * GH + j - WEIGH_LAG)
                                if g < groups_max and k == MAX_SPAN[g][1]:
                                    pe_max_rows(pe, g + 1)
                                for n in STEPS_AT.get(i, ()) if following else ():
                                    pe_step(pe, n, STEP_BANKS)
                        for n in range(NG * KT * GH - WEIGH_LAG, NG * KT * GH):
                            weigh(n)
                        if following:
                            pe_max_rows(pe, NG)

                    flag = pe.value_load(any_masked[0:1, 0:1], min_val=0, max_val=1)
                    with pe.If(flag > 0):
                        groups(masked=True)
                    with pe.Else():
                        groups(masked=False)

                @block.scalar
                def _(act):
                    def take_outputs(g):
                        act.wait_ge(S["s_pv"], (g + 1) * KT * GH)
                        nc.scalar.copy(oT_sb[:, g, :], ps[:, OUT_BANK, :]).then_inc(S["s_oTs"], 1)

                    for g in range(NG):
                        for k in range(KT):
                            i = g * KT + k
                            if g < NG - 1 and k == MAX_SPAN[g][1] + 1:
                                act_max_rows(act, g + 1, (g + 1) % 2)
                            for j in range(GH):
                                n = i * GH + j
                                act.wait_ge(S["s_st"], n + 1)
                                if n >= PRING:
                                    act.wait_ge(S["s_pv"], n - PRING + 1)
                                nc.scalar.activation(probs[0:KW[k], n % PRING, :], ps[0:KW[k], 4 + n % 3, :], ACT.Exp,
                                                     scale=HD ** -0.5).then_inc(S["s_exp"], 1)
                            if k == 0 and g:
                                take_outputs(g - 1)
                            if following:
                                for n in STEPS_AT.get(i - 1, ()):
                                    act_step(act, n, STEP_BANKS)
                                for n in STEPS_AT.get(i - 3, ()):
                                    if STEPS[n][0] == "piece":
                                        act_second(act, n)
                    take_outputs(NG - 1)
                    if following:
                        act_max_rows(act, NG, 0)

                @block.gpsimd
                def _(pool):
                    if following:
                        for t in range(TT - 1):
                            pool_mask(pool, t)
                        rsqrt(pool, 0)
                        for i in range(2):
                            pool_third(pool, i)
                        rsqrt(pool, 1)
                        for i in range(2, 4):
                            pool_third(pool, i)
                        pool_mask(pool, TT - 1)
                        for i in range(4, PIECES):
                            pool_third(pool, i)

                @block.vector
                def _(dve):
                    link = Link(dve)
                    for g in range(NG):
                        for k in range(KT):
                            i = g * KT + k
                            for n in chunk_range(g, k):
                                if g == NG - 1 and n % GROUP_CHUNKS == 0:
                                    dve.wait_ge(S["s_bias"], TT)
                                dve_max(dve, n, bias if g < NG - 1 else bias_next)
                            if g < groups_max and k == MAX_SPAN[g][1] - 1:
                                dve_max_parts(dve, link, g + 1)
                            if following:
                                for n in STEPS_AT.get(i - 2, ()):
                                    dve_step(dve, link, n, STEP_BANKS)
                                if 0 <= i - NORMS_AT < NORM_PARTS:
                                    dve_norms(dve, link, i - NORMS_AT)
                    if following:
                        dve_step(dve, link, len(STEPS) - 1, STEP_BANKS)

        def hand_over(act):
            nc.scalar.copy(v_aug[:, 0:KT - 1, :, 0:HD], v_next[:, 0:KT - 1, :].rearrange("p k (h d) -> p k h d", h=H)).then_inc(S["s_next"], 1)
            nc.scalar.copy(v_aug[0:KW[-1], KT - 1, :, 0:HD],
                           v_next[0:KW[-1], KT - 1, :].rearrange("p (h d) -> p h d", h=H)).then_inc(S["s_next"], 1)

        def hand_over_rest(act):
            nc.scalar.copy(bias[:].rearrange("p t n -> p (t n)"), bias_next[:].rearrange("p t n -> p (t n)")).then_inc(S["s_next"], 1)
            nc.scalar.copy(x1_sb[:].rearrange("p t d -> p (t d)"), x1_next[:].rearrange("p t d -> p (t d)")).then_inc(S["s_next"], 1)
            act.wait_ge(S["s_next"], 4)

        def project(row, next_batch, following):
            with nc.Block(no_gpsimd_drain=True) as block:
                @block.sync
                def _(sp):
                    if following:
                        load_group(sp, 1, 1, next_batch)
                    sp.wait_ge(S["s_x2"], 1)
                    sp.dma_start(x2_dram[row, :].rearrange("(t p) d -> p t d", p=P), x2_sb).then_inc(S["s_x2_out"], 16)
                    if following:
                        sp.wait_ge(s_kl[1], 32 * 2)
                    sp.wait_ge(S["s_x2_out"], 16)

                @block.tensor
                def _(pe):
                    for t in range(TT):
                        for g in range(NG):
                            last = nc.tensor.transpose(ps[:, t, g * P:(g + 1) * P], oT_sb[:, g, t * P:(t + 1) * P], ident[:])
                        last.then_inc(S["s_tr"], 1)
                    for t in range(TT):
                        pe.wait_ge(S["s_on"], t + 1)
                        for c in range(DC):
                            last = nc.tensor.transpose(ps[:, 4 + t, c * P:(c + 1) * P], on_sb[:, t, c * P:(c + 1) * P], ident[:])
                        last.then_inc(S["s_tr2"], 1)
                    for t in range(TT):
                        pe.wait_ge(S["s_onT"], t + 1)
                        for c in range(DC):
                            last = nc.tensor.matmul(ps[:, t, 0:D], onT_sb[:, c, t * P:(t + 1) * P], wo_sb[:, c, :],
                                                    start=(c == 0), stop=(c == DC - 1))
                        last.then_inc(S["s_y"], 1)

                @block.scalar
                def _(act):
                    if following:
                        hand_over(act)
                    for t in range(TT):
                        act.wait_ge(S["s_tr2"], t + 1)
                        nc.scalar.copy(onT_sb[:, :, t * P:(t + 1) * P],
                                       ps[:, 4 + t, 0:D].rearrange("p (c q) -> p c q", c=DC)).then_inc(S["s_onT"], 1)
                    if following:
                        act.wait_ge(S["s_residual"], 1)
                        hand_over_rest(act)

                @block.gpsimd
                def _(pool):
                    rsqrt(pool, 2 if following else 0)

                @block.vector
                def _(dve):
                    link = Link(dve)
                    link.n = DVE_ATTEND + (DVE_PREPARE if following else -5)
                    for t in range(TT):
                        dve.wait_ge(S["s_tr"], t + 1)
                        heads = ps[:, t, :].rearrange("p (h d) -> p h d", h=H)
                        link(nc.vector.reciprocal(rsum[:, t, :], heads[:, :, HD]))
                        nc.vector.tensor_tensor(on_sb[:, t, :].rearrange("p (h d) -> p h d", h=H), heads[:, :, 0:HD],
                                                rsum[:, t, :].rearrange("p (h a) -> p h a", a=1).to_broadcast([P, H, HD]),
                                                ALU.mult).then_inc(S["s_on"], 1)
                    for t in range(TT):
                        dve.wait_ge(S["s_y"], t + 1)
                        link(nc.vector.tensor_tensor(u_sb[:, t, :], ps[:, t, 0:D], bo_sb[:], ALU.add))
                    nc.vector.tensor_tensor(u_sb[:], u_sb[:], x1_sb[:], ALU.add).then_inc(S["s_residual"], 1)
                    dve.wait_ge(S["s_residual"], 1)
                    norm_stats(link, dve, u_sb)
                    norm_apply(link, dve, 3 if following else 1, u_sb, x2_sb)
                    nc.vector.engine_nop().then_inc(S["s_x2"], 1)

        with nc.Block(no_gpsimd_drain=True) as block:
            @block.sync
            def _(sp):
                def mask_row(t):
                    return slice(t * P, (t + 1) * P)

                load_rows(sp, slice(0, T), mask_row)
                load_ctx(sp, slice(0, D))
                for t in range(1, 2):
                    load_mask(sp, mask_row, t)
                for i in range(6):
                    store_piece(sp, i, slice(0, 1))
                load_mask(sp, mask_row, 2)
                for i in range(6, PIECES):
                    store_piece(sp, i, slice(0, 1))
                stores_done(sp)
                for g in range(2):
                    load_group(sp, g, g, slice(0, 1))
                load_mask(sp, mask_row, 3)
                for slot in range(2):
                    sp.wait_ge(s_kl[slot], 32)

            @block.tensor
            def _(pe):
                for n in range(len(STEPS) - 1):
                    pe_step(pe, n, FIRST_BANKS)
                pe.wait_ge(s_kl[0], 32)
                for n in range(GROUP_CHUNKS):
                    pe_max(pe, n, 0)
                pe_max_rows(pe, 1)
                pe_step(pe, len(STEPS) - 1, FIRST_BANKS)

            @block.scalar
            def _(act):
                for n in range(len(STEPS)):
                    act_step(act, n, FIRST_BANKS)
                    if n and STEPS[n - 1][0] == "piece":
                        act_second(act, n - 1)
                act.wait_ge(S["s_vx_sb"], -(-KT // 2))
                hand_over(act)
                act_max_rows(act, 1, 0)
                act.wait_ge(S["s_bias"], TT)
                hand_over_rest(act)

            @block.gpsimd
            def _(pool):
                pool_mask(pool, 0)
                rsqrt(pool, 0)
                rsqrt(pool, 1)
                for i in range(4):
                    pool_third(pool, i)
                pool_mask(pool, 1)
                for i in range(4, PIECES):
                    pool_third(pool, i)
                pool_mask(pool, 2)
                pool_mask(pool, 3)

            @block.vector
            def _(dve):
                link = Link(dve)
                for n in range(len(STEPS) - 1):
                    dve_step(dve, link, n, FIRST_BANKS)
                    if STEPS[n][:2] == ("o", 1):
                        for part in range(NORM_PARTS):
                            dve_norms(dve, link, part)
                for n in range(GROUP_CHUNKS):
                    if n % 16 == 0:
                        dve.wait_ge(S["s_bias"], n // 16 + 1)
                    dve_max(dve, n, bias_next)
                dve_max_parts(dve, link, 1)
                dve_step(dve, link, len(STEPS) - 1, FIRST_BANKS)

        nc.all_engine_barrier(sems_to_clear=as_range(per_batch.values()))

        with nc.Fori(0, B - 1) as b:
            attend(bass.ds(b, 1), bass.ds(b * T + T, T), lambda t: bass.ds(b * T + (T + t * P), P),
                   bass.ds(b * D + D, D), bass.ds(b + 1, 1), following=True)
            project(bass.ds(b * T, T), bass.ds(b + 1, 1), following=True)
            nc.all_engine_barrier(sems_to_clear=as_range(per_batch.values()))
        attend(slice(B - 1, B), None, None, None, None, following=False)
        project(slice((B - 1) * T, B * T), None, following=False)


DVE_NORM = 3 * TT
DVE_PREPARE = 2 * DVE_NORM + 3 + 1
DVE_ATTEND = 5 * NG


def mixture(nc, x2_dram, ident, ps, router_wT, correction, up_w, down_w, out):
    with ExitStack() as ctx:
        def sb(name, shape, dt=F32):
            return ctx.enter_context(nc.sbuf_tensor(name, shape, dt))

        x2 = sb("x2", [P, NT, D])
        x2T = sb("x2T", [P, 2, DC, NT * P], F32R)
        router_sb = sb("router_sb", [P, DC, E])
        router_hl = sb("router_hl", [P, 2, DC, E], F32R)
        corr_sb = sb("corr_sb", [P, E])
        lower = sb("lower", [P, G, G])
        power = sb("power_m", [P, NT])
        scores = sb("scores", [P, NT, E])
        sfc = sb("sfc", [P, NT, E])
        work = sb("work", [P, NT, E])
        work2 = sb("work2", [P, NT, E])
        m1 = sb("m1", [P, NT * G])
        m2 = sb("m2", [P, NT * G])
        cnt = sb("cnt", [P, NT * G])
        top8 = sb("top8", [P, NT, K_TOP])
        total = sb("total", [P, NT])
        combine = sb("combine", [P, NT, EXPERTS])
        w_in = sb("w_in", [P, 2, 2 * D])
        w_hl = sb("w_hl", [P, 2, 2, 2 * D], F32R)
        hr = sb("hr", [P, 4, 512])
        hs = sb("hs", [P, 4, 512])
        h2 = sb("h2", [P, 2, 2, NT * P], F32R)
        result = sb("result", [P, NT, D])
        stats = sb("stats_m", [P, NT, 6])
        mv = sb("mv_m", [P, NT, 2])
        ve = sb("ve_m", [P, NT])
        rstd = sb("rstd_m", [P, NT])

        S = semaphores(ctx, nc, "r_x0 r_x1 r_x2 r_x3 r_load r_const0 r_const r_router r_xT r_xTs r_xTl r_logit r_exp r_dve "
                                "s_wu0 s_wu1 s_wd0 s_wd1 s_up_hi s_up_lo s_down_hi s_down_lo s_up s_relu s_square s_h_hi s_h_lo "
                                "s_y2 s_y_free s_var2 s_rstd2 s_final s_store")

        with nc.Block(no_gpsimd_drain=True) as block:
            @block.sync
            def _(sp):
                for q in range(B):
                    sp.dma_start(x2[:, q * TT:(q + 1) * TT, :],
                                 x2_dram[q * T:(q + 1) * T, :].rearrange("(t p) d -> p t d", p=P)).then_inc(S[f"r_x{q}"], 16)
                sp.dma_start(router_sb[:], router_wT.rearrange("(c p) n -> p c n", p=P)).then_inc(S["r_load"], 16)
                sp.dma_start(corr_sb[:], correction.rearrange("(a n) -> a n", a=1).to_broadcast([P, E])).then_inc(S["r_load"], 16)

            @block.gpsimd
            def _(pool):
                nc.gpsimd.memset(lower[:], 1.0).then_inc(S["r_const0"], 1)
                nc.gpsimd.memset(power[:], -0.5).then_inc(S["r_const0"], 1)
                nc.gpsimd.memset(combine[:], 1.0).then_inc(S["r_const0"], 1)
                pool.wait_ge(S["r_const0"], 3)
                nc.gpsimd.affine_select(out=lower[:], in_=lower[:], compare_op=ALU.is_gt, fill=0.0,
                                        base=0, pattern=[[1, G], [-1, G]], channel_multiplier=0).then_inc(S["r_const"], 1)

            @block.tensor
            def _(pe):
                for t in range(NT):
                    if t % TT == 0:
                        pe.wait_ge(S[f"r_x{t // TT}"], 16)
                    if t >= 4:
                        pe.wait_ge(S["r_xTl"], t - 3)
                    for c in range(DC):
                        last = nc.tensor.transpose(ps[:, 4 + t % 4, c * P:(c + 1) * P], x2[:, t, c * P:(c + 1) * P], ident[:])
                    last.then_inc(S["r_xT"], 1)
                pe.wait_ge(S["r_load"], 32)
                pe.wait_ge(S["r_router"], 2)
                for t in range(NT):
                    pe.wait_ge(S["r_xTl"], t + 1)
                    for n, (a, w, c) in enumerate(PASSES):
                        last = nc.tensor.matmul(ps[:, t // 8, (t % 8) * E:(t % 8 + 1) * E], x2T[:, a, c, t * P:(t + 1) * P],
                                                router_hl[:, w, c, :], start=(n == 0), stop=(n == len(PASSES) - 1))
                last.then_inc(S["r_logit"], 1)

            @block.scalar
            def _(act):
                for t in range(NT):
                    act.wait_ge(S["r_xT"], t + 1)
                    nc.scalar.copy(x2T[:, 0, :, t * P:(t + 1) * P],
                                   ps[:, 4 + t % 4, 0:D].rearrange("p (c q) -> p c q", c=DC)).then_inc(S["r_xTs"], 1)
                act.wait_ge(S["r_logit"], 1)
                nc.scalar.activation(work[:].rearrange("p t e -> p (t e)"), ps[:, 0:2, :].rearrange("p a b -> p (a b)"),
                                     ACT.Exp, scale=-1.0).then_inc(S["r_exp"], 1)

            @block.vector
            def _(dve):
                n = [0]

                def link(ins):
                    n[0] += 1
                    ins.then_inc(S["r_dve"], 1)
                    dve.wait_ge(S["r_dve"], n[0])

                def by_group(ap):
                    return ap[:].rearrange("p t (g e) -> p (t g) e", g=G)

                def over(ap, k):
                    return ap.rearrange("p (n a) -> p n a", a=1).to_broadcast([P, ap.shape[1], k])

                dve.wait_ge(S["r_load"], 32)
                nc.vector.tensor_copy(router_hl[:, 0, :, :], router_sb[:]).then_inc(S["r_router"], 1)
                dve.wait_ge(S["r_router"], 1)
                nc.vector.tensor_tensor(router_hl[:, 1, :, :], router_sb[:], router_hl[:, 0, :, :].bitcast(F32),
                                        ALU.subtract).then_inc(S["r_router"], 1)
                for t in range(NT):
                    dve.wait_ge(S["r_xTs"], t + 1)
                    nc.vector.tensor_tensor(x2T[:, 1, :, t * P:(t + 1) * P],
                                            ps[:, 4 + t % 4, 0:D].rearrange("p (c q) -> p c q", c=DC),
                                            x2T[:, 0, :, t * P:(t + 1) * P].bitcast(F32), ALU.subtract).then_inc(S["r_xTl"], 1)
                dve.wait_ge(S["r_exp"], 1)
                link(nc.vector.tensor_scalar(work[:], work[:], 1.0, None, ALU.add))
                link(nc.vector.reciprocal(scores[:], work[:]))
                link(nc.vector.tensor_tensor(sfc[:], scores[:], corr_sb[:].rearrange("p (a e) -> p a e", a=1).to_broadcast([P, NT, E]), ALU.add))
                link(nc.vector.tensor_reduce(m1[:], by_group(sfc), AX.X, ALU.max))
                link(nc.vector.tensor_tensor(by_group(work), by_group(sfc), over(m1[:], E // G), ALU.is_equal))
                link(nc.vector.tensor_reduce(cnt[:], by_group(work), AX.X, ALU.add))
                link(nc.vector.scalar_tensor_tensor(out=work2[:], in0=work[:], scalar=LOWEST, in1=sfc[:], op0=ALU.mult, op1=ALU.add))
                link(nc.vector.tensor_reduce(m2[:], by_group(work2), AX.X, ALU.max))
                link(nc.vector.tensor_scalar(cnt[:], cnt[:], 1.5, 1.0, ALU.is_gt, ALU.subtract))
                link(nc.vector.scalar_tensor_tensor(out=cnt[:], in0=cnt[:], scalar=-LOWEST, in1=m1[:], op0=ALU.mult, op1=ALU.add))
                link(nc.vector.tensor_tensor(m2[:], m2[:], cnt[:], ALU.max))
                link(nc.vector.tensor_tensor(m1[:], m1[:], m2[:], ALU.add))
                others = m1[:].rearrange("p (t a g) -> p t a g", a=1, g=G).to_broadcast([P, NT, G, G])
                itself = m1[:].rearrange("p (t g a) -> p t g a", a=1, g=G).to_broadcast([P, NT, G, G])
                w4 = work[:].rearrange("p t (g e) -> p t g e", g=G)
                v4 = work2[:].rearrange("p t (g e) -> p t g e", g=G)
                dve.wait_ge(S["r_const"], 1)
                link(nc.vector.tensor_tensor(w4, others, itself, ALU.is_gt))
                link(nc.vector.tensor_tensor(v4, others, itself, ALU.is_equal))
                link(nc.vector.tensor_tensor(v4, v4, lower[:].rearrange("p (a g) e -> p a g e", a=1).to_broadcast([P, NT, G, G]), ALU.mult))
                link(nc.vector.tensor_tensor(work[:], work[:], work2[:], ALU.add))
                link(nc.vector.tensor_reduce(cnt[:], by_group(work), AX.X, ALU.add))
                link(nc.vector.tensor_scalar(cnt[:], cnt[:], TOPK_GROUP - 0.5, None, ALU.is_lt))
                link(nc.vector.tensor_tensor(by_group(work), by_group(sfc), over(cnt[:], E // G), ALU.mult))
                for t in range(NT):
                    link(nc.vector.max(top8[:, t, :], work[:, t, :]))
                    link(nc.vector.match_replace(work2[:, t, :], top8[:, t, :], work[:, t, :], LOWEST))
                link(nc.vector.tensor_scalar(work2[:], work2[:], LOWEST / 2, None, ALU.is_lt))
                link(nc.vector.tensor_tensor(work2[:], work2[:], scores[:], ALU.mult))
                link(nc.vector.tensor_reduce(total[:], work2[:], AX.X, ALU.add))
                link(nc.vector.tensor_scalar(total[:], total[:], 1e-20, None, ALU.add))
                link(nc.vector.reciprocal(total[:], total[:]))
                link(nc.vector.tensor_tensor(work2[:], work2[:], over(total[:], E), ALU.mult))
                link(nc.vector.tensor_scalar(combine[:, :, 0:E], work2[:], ROUTE_SCALE, None, ALU.mult))

        PAIRS = NT // 2
        up_v = up_w.rearrange("e (c p) i -> p e c i", p=P)
        down_v = down_w.rearrange("e i d -> i e d")
        s_wu, s_wd = [S["s_wu0"], S["s_wu1"]], [S["s_wd0"], S["s_wd1"]]
        LOOPS = EXPERTS // 2

        with nc.Block(no_gpsimd_drain=True) as block:
            @block.sync
            def _(sp):
                def load_up(k, s):
                    sp.dma_start(w_in[:, s:s + 1, 0:D].rearrange("p s (c i) -> p s c i", c=DC), up_v[:, k, :, :]).then_inc(s_wu[s], 16)

                def load_down(k, s):
                    sp.dma_start(w_in[:, s:s + 1, D:2 * D], down_v[:, k, :]).then_inc(s_wd[s], 16)

                for s in range(2):
                    load_up(slice(s, s + 1), s)
                    load_down(slice(s, s + 1), s)
                with sp.Fori(1, LOOPS) as i:
                    for s in range(2):
                        sp.wait_ge(S["s_up_lo"], i * 2 + (s - 1))
                        load_up(bass.ds(i * 2 + s, 1), s)
                        sp.wait_ge(S["s_down_lo"], i * 2 + (s - 1))
                        load_down(bass.ds(i * 2 + s, 1), s)
                out_v = out.rearrange("(t p) d -> p t d", p=P)
                for q in range(4):
                    sp.wait_ge(S["s_final"], 4 * q + 4)
                    sp.dma_start(out_v[:, 4 * q:4 * q + 4, :], result[:, 4 * q:4 * q + 4, :]).then_inc(S["s_store"], 16)
                sp.wait_ge(S["s_store"], 64)

            @block.tensor
            def _(pe):
                def up(k, s, first=False):
                    pe.wait_ge(S["s_up_lo"], k + 1)
                    for q in range(4):
                        if not first:
                            pe.wait_ge(S["s_relu"], k * 4 + (q - 3))
                        for n, (a, w, c) in enumerate(PASSES):
                            last = nc.tensor.matmul(ps[:, q, :], w_hl[:, s, w, c * I_MOE:(c + 1) * I_MOE],
                                                    x2T[:, a, c, q * 512:(q + 1) * 512],
                                                    start=(n == 0), stop=(n == len(PASSES) - 1))
                        last.then_inc(S["s_up"], 1)

                def down(k, s):
                    pe.wait_ge(S["s_down_lo"], k + 1)
                    for r in range(PAIRS):
                        if r % 2 == 0:
                            pe.wait_ge(S["s_h_lo"], k * 4 + (r // 2 + 1))
                        pe.wait_ge(S["s_y_free"], k * PAIRS + (r + 1))
                        for u in range(2):
                            t = 2 * r + u
                            for n, (a, w) in enumerate(((0, 0), (0, 1), (1, 0))):
                                last = nc.tensor.matmul(ps[:, 4 + r % 4, u * D:(u + 1) * D], h2[:, s, a, t * P:(t + 1) * P],
                                                        w_hl[:, s, w, D:2 * D], start=(n == 0), stop=(n == 2))
                        last.then_inc(S["s_y2"], 1)

                up(0, 0, first=True)
                with pe.Fori(0, LOOPS - 1) as i:
                    up(i * 2 + 1, 1)
                    down(i * 2, 0)
                    up(i * 2 + 2, 0)
                    down(i * 2 + 1, 1)
                up(EXPERTS - 1, 1)
                down(EXPERTS - 2, 0)
                down(EXPERTS - 1, 1)

            @block.scalar
            def _(act):
                def up_high(k, s, load, first=False):
                    act.wait_ge(s_wu[s], load * 16)
                    if not first:
                        act.wait_ge(S["s_up"], k * 4 - 4)
                    nc.scalar.copy(w_hl[:, s, 0, 0:D], w_in[:, s, 0:D]).then_inc(S["s_up_hi"], 1)

                def relu(k, q, first):
                    if not (first and k == 0):
                        act.wait_ge(S["s_square"], k * 4 + (q - 3))
                    act.wait_ge(S["s_up"], k * 4 + (q + 1))
                    nc.scalar.activation(hr[:, q, :], ps[:, q, :], ACT.Relu).then_inc(S["s_relu"], 1)

                def high(k, s, q):
                    act.wait_ge(S["s_square"], k * 4 + (q + 1))
                    nc.scalar.copy(h2[:, s, 0, q * 512:(q + 1) * 512], hs[:, q, :]).then_inc(S["s_h_hi"], 1)

                def down_high(k, s, load, first):
                    act.wait_ge(s_wd[s], load * 16)
                    if not first:
                        act.wait_ge(S["s_y2"], k * PAIRS - PAIRS)
                    nc.scalar.copy(w_hl[:, s, 0, D:2 * D], w_in[:, s, D:2 * D]).then_inc(S["s_down_hi"], 1)

                def hidden(k, s, load, first=False):
                    relu(k, 0, first)
                    relu(k, 1, first)
                    high(k, s, 0)
                    relu(k, 2, first)
                    high(k, s, 1)
                    relu(k, 3, first)
                    high(k, s, 2)
                    down_high(k, s, load, first)
                    high(k, s, 3)

                up_high(0, 0, 1, first=True)
                up_high(1, 1, 1, first=True)
                hidden(0, 0, 1, first=True)
                up_high(2, 0, 2)
                hidden(1, 1, 1, first=True)
                with act.Fori(1, LOOPS - 1) as i:
                    up_high(i * 2 + 1, 1, i + 1)
                    hidden(i * 2, 0, i + 1)
                    up_high(i * 2 + 2, 0, i + 2)
                    hidden(i * 2 + 1, 1, i + 1)
                up_high(EXPERTS - 1, 1, LOOPS)
                hidden(EXPERTS - 2, 0, LOOPS)
                hidden(EXPERTS - 1, 1, LOOPS)

            @block.gpsimd
            def _(pool):
                def low(k, s, columns, s_high, s_low):
                    pool.wait_ge(s_high, k + 1)
                    nc.gpsimd.tensor_tensor(w_hl[:, s, 1, columns], w_in[:, s, columns], w_hl[:, s, 0, columns].bitcast(F32),
                                            ALU.subtract).then_inc(s_low, 1)

                def up_low(k, s):
                    low(k, s, slice(0, D), S["s_up_hi"], S["s_up_lo"])

                def square(k, s, first=False):
                    for q in range(4):
                        pool.wait_ge(S["s_relu"], k * 4 + (q + 1))
                        if not first:
                            pool.wait_ge(S["s_h_lo"], k * 4 + (q - 3))
                        nc.gpsimd.tensor_tensor(hs[:, q, :], hr[:, q, :], hr[:, q, :], ALU.mult).then_inc(S["s_square"], 1)
                    low(k, s, slice(D, 2 * D), S["s_down_hi"], S["s_down_lo"])

                up_low(0, 0)
                up_low(1, 1)
                square(0, 0, first=True)
                with pool.Fori(1, LOOPS) as i:
                    up_low(i * 2, 0)
                    square(i * 2 - 1, 1)
                    up_low(i * 2 + 1, 1)
                    square(i * 2, 0)
                square(EXPERTS - 1, 1)
                pool.wait_ge(S["s_var2"], 1)
                nc.gpsimd.tensor_tensor(rstd[:], ve[:], power[:], ALU.pow).then_inc(S["s_rstd2"], 1)

            @block.vector
            def _(dve):
                dve.sem_inc(S["s_y_free"], 4)
                def low(k, s, q):
                    dve.wait_ge(S["s_h_hi"], k * 4 + (q + 1))
                    nc.vector.tensor_tensor(h2[:, s, 1, q * 512:(q + 1) * 512], hs[:, q, :],
                                            h2[:, s, 0, q * 512:(q + 1) * 512].bitcast(F32), ALU.subtract).then_inc(S["s_h_lo"], 1)

                def add(k, r):
                    dve.wait_ge(S["s_y2"], k * PAIRS + (r + 1))
                    for u in range(2):
                        t = 2 * r + u
                        last = nc.vector.scalar_tensor_tensor(
                            out=x2[:, t, :], in0=ps[:, 4 + r % 4, u * D:(u + 1) * D],
                            scalar=combine[:, t, k:k + 1] if isinstance(k, int) else combine[:, t, bass.ds(k, 1)],
                            in1=x2[:, t, :], op0=ALU.mult, op1=ALU.add)
                    last.then_inc(S["s_y_free"], 1)

                def step(k, s):
                    for r in range(PAIRS):
                        add(k, r)
                    for q in range(4):
                        low(k + 1, s, q)

                for q in range(4):
                    low(0, 0, q)
                with dve.Fori(0, LOOPS - 1) as i:
                    step(i * 2, 1)
                    step(i * 2 + 1, 0)
                step(EXPERTS - 2, 1)
                for r in range(PAIRS):
                    add(EXPERTS - 1, r)
                dve.wait_ge(S["s_y_free"], EXPERTS * PAIRS + 4)
                base = [DVE_ROUTE]

                def counted(ins):
                    base[0] += 1
                    ins.then_inc(S["r_dve"], 1)
                for t in range(NT):
                    counted(nc.vector.bn_stats(stats[:, t, :], x2[:, t, :]))
                dve.wait_ge(S["r_dve"], base[0])
                for t in range(NT):
                    counted(nc.vector.bn_aggr(mv[:, t, :], stats[:, t, :]))
                dve.wait_ge(S["r_dve"], base[0])
                nc.vector.tensor_scalar(ve[:], mv[:, :, 1], EPS, None, ALU.add).then_inc(S["s_var2"], 1)
                dve.wait_ge(S["s_rstd2"], 1)
                for t in range(NT):
                    nc.vector.tensor_scalar(result[:, t, :], x2[:, t, :], mv[:, t, 0:1], rstd[:, t:t + 1],
                                            ALU.subtract, ALU.mult).then_inc(S["s_final"], 1)


DVE_ROUTE = 19 + 2 * NT + 7


def kernel(x, ctx_1024, mask_Bx1xSxS2_if1, L0_attn_W_qkv, L0_attn_b_qkv, L0_attn_ln_w, L0_attn_ln_b,
           L0_xattn_Wq, L0_xattn_Wk, L0_xattn_Wv, L0_xattn_Wo, L0_xattn_bo, L0_ffn_router_w,
           L0_ffn_correction_bias, L0_ffn_up_w, L0_ffn_down_w, L0_ffn_shared_up_w, L0_ffn_shared_down_w):
    import numpy as np
    import concourse.bacc as bacc
    from concourse.bass_utils import run_bass_kernel_spmd

    x_rows = np.asarray(x).reshape(B * T, D)
    shared_up = np.asarray(L0_ffn_shared_up_w).reshape(D, EXPERTS - E, I_MOE).transpose(1, 0, 2)
    shared_down = np.asarray(L0_ffn_shared_down_w).reshape(EXPERTS - E, I_MOE, D)

    def by_width(w):
        return np.asarray(w).reshape(H, HD, D).transpose(2, 1, 0).reshape(D, D)

    given = {
        "x": x_rows, "xT": x_rows.T,
        "ctxT": np.asarray(ctx_1024).transpose(0, 2, 1).reshape(B * D, S2),
        "mask": np.asarray(mask_Bx1xSxS2_if1).reshape(B * T, S2),
        "w_qkv": L0_attn_W_qkv, "b_qkv": L0_attn_b_qkv, "ln_w": L0_attn_ln_w, "ln_b": L0_attn_ln_b,
        "wqT": by_width(L0_xattn_Wq), "wkT": by_width(L0_xattn_Wk),
        "wvT": np.asarray(L0_xattn_Wv).T, "woT": np.asarray(L0_xattn_Wo).T, "bo": L0_xattn_bo,
        "router_wT": np.asarray(L0_ffn_router_w).T, "correction": L0_ffn_correction_bias,
        "up_w": np.concatenate([np.asarray(L0_ffn_up_w), shared_up]),
        "down_w": np.concatenate([np.asarray(L0_ffn_down_w), shared_down]),
    }
    nc = bacc.Bacc("TRN2", target_bir_lowering=False, num_devices=1)
    arrays, args = {}, []
    for name, a in given.items():
        a = np.ascontiguousarray(a)
        arrays[f"in_{name}"] = a
        args.append(nc.dram_tensor(f"in_{name}", a.shape, mybir.dt.from_np(a.dtype), kind="ExternalInput").ap())
    args.append(nc.dram_tensor("out_dram", (B * T, D), F32, kind="ExternalOutput").ap())
    decoder_layer(nc, *args)
    r = run_bass_kernel_spmd(nc, [arrays], core_ids=[0])
    return r.results[0]["out_dram"].reshape(B, T, D)
```

```python
import concourse.bass as bass
from concourse import mybir
from contextlib import ExitStack

F32, BF16, I32 = mybir.dt.float32, mybir.dt.bfloat16, mybir.dt.int32
F32R = mybir.dt.float32r
ALU, ACT, AX = mybir.AluOpType, mybir.ActivationFunctionType, mybir.AxisListType

P = 128
B, T, D = 4, 512, 256
S2 = 1601
H, HD = 16, 16
SPAN = 64
E, I_MOE, I_SHARED = 64, 128, 512
EXPERTS = E + I_SHARED // I_MOE
G, TOPK_GROUP, K_TOP = 8, 4, 8
ROUTE_SCALE = 2.5
EPS = 1e-5
MASKED = -1e20
LOWEST = -1e30

DC = D // P
TT = T // P
NT = B * TT
KT = -(-S2 // P)
KW = [min(P, S2 - P * k) for k in range(KT)]
CHUNKS = [(c, min(512, S2 - c)) for c in range(0, S2, 512)]
GH = 4
NG = H // GH
TERMS = [(0, 0), (0, 1), (0, 2), (1, 0), (1, 1), (2, 0)]
ROWS = len(TERMS) * HD
MROWS = 3
K_ROWS = [(0, 3, 0), (3, 2, 0), (5, 1, 0)]
Q_ROWS = [(0, 3, 0), (3, 2, 1), (5, 1, 2)]
PASSES = [(a, w, c) for a, w in ((0, 0), (0, 1), (1, 0)) for c in range(DC)]
MAX_CHUNKS = [(c, min(401, S2 - c)) for c in range(0, S2, 401)]
GROUP_CHUNKS = len(MAX_CHUNKS) * TT * GH
WEIGH_LAG = 2
TWO_ONES = 1 + 0x3F80 / 2 ** 23
SLOTS = 3
SLOT = [0, 1, 2, 1, 0]
PRING = 8
SRING = 3
OUT_BANK = 7

PROJ = [(False, 0, c, w) for c, w in CHUNKS] + [(True, m, 0, T) for m in range(DC)] + [(False, 1, c, w) for c, w in CHUNKS]
PIECES = len(PROJ)
STEPS = ([("qk", m) for m in range(2 * DC)] + [("v", 0), ("v", 1), ("band", 0), ("band", 1), ("o", 0), ("o", 1)]
         + [("piece", i, *PROJ[i]) for i in range(4)] + [("x1T", 0), ("x1T", 1)]
         + [("piece", i, *PROJ[i]) for i in range(4, PIECES)]
         + [("vx", i) for i in range(-(-KT // 2))] + [("any", 0)])
PIECE_STEPS = [n for n, step in enumerate(STEPS) if step[0] == "piece"]
MAX_BANKS = 3
SCORE_BANKS = [4, 5]
STEP_BANKS = [3, 6]
FIRST_BANKS = [3, 4, 5, 6, 7]
STEP_TILES = [1, 2, 3, 4, 5, 5, 7, 7, 9, 10, 11, 13, 15, 17, 18, 19, 21, 22, 24, 26, 28, 30,
              32, 34, 35, 37, 38, 39, 49, 50]
assert len(STEP_TILES) == len(STEPS)
STEPS_AT = {tile: [n for n, at in enumerate(STEP_TILES) if at == tile] for tile in STEP_TILES}
NORM_PARTS = 4
NORMS_AT = {11: [0], 12: [1], 15: [2], 16: [3]}
MAX_SPAN = [(0, 11), (0, 11), (1, 11), (0, 13)]


def semaphores(ctx, nc, names):
    return {n: ctx.enter_context(nc.semaphore(n)) for n in names.split()}


def as_range(sems):
    numbers = sorted(s.num for s in sems)
    assert numbers == list(range(numbers[0], numbers[0] + len(numbers)))
    return range(numbers[0], numbers[-1] + 1)


def decoder_layer(nc, x, xT, ctxT, mask, w_qkv, b_qkv, ln_w, ln_b, wqT, wkT, wvT, woT, bo,
                  router_wT, correction, up_w, down_w, out):
    k_dram = nc.dram_tensor("k_dram", (B, ROWS, H, S2), BF16).ap()
    q_dram = nc.dram_tensor("q_dram", (B, ROWS, H, T), BF16).ap()
    x2_dram = nc.dram_tensor("x2_dram", (B * T, D), F32).ap()

    with ExitStack() as ctx:
        ident = ctx.enter_context(nc.sbuf_tensor("ident", [P, P], F32))
        ident_bf = ctx.enter_context(nc.sbuf_tensor("ident_bf", [P, P], BF16))
        ps = ctx.enter_context(nc.psum_tensor("ps", [P, 8, 512], F32))

        attention(nc, ident, ident_bf, ps, k_dram, q_dram, x2_dram, x, xT, ctxT, mask,
                  w_qkv, b_qkv, ln_w, ln_b, wqT, wkT, wvT, woT, bo)
        mixture(nc, x2_dram, ident, ps, router_wT, correction, up_w, down_w, out)


def attention(nc, ident, ident_bf, ps, k_dram, q_dram, x2_dram, x, xT, ctxT, mask,
              w_qkv, b_qkv, ln_w, ln_b, wqT, wkT, wvT, woT, bo):
    with ExitStack() as ctx:
        def sb(name, shape, dt=F32):
            return ctx.enter_context(nc.sbuf_tensor(name, shape, dt))

        band = sb("band", [P, 2 * P])
        w_qkv_sb = sb("w_qkv_sb", [P, DC, 3 * D])
        wq_sb = sb("wq_sb", [P, DC, D])
        wk_sb = sb("wk_sb", [P, DC, D])
        wv_sb = sb("wv_sb", [P, DC, D])
        wo_sb = sb("wo_sb", [P, DC, D])
        qk_bias = sb("qk_bias", [P, 2 * DC])
        v_bias = sb("v_bias", [P, D])
        lnw_sb = sb("lnw_sb", [P, D])
        lnb_sb = sb("lnb_sb", [P, D])
        bo_sb = sb("bo_sb", [P, D])
        power = sb("power", [P, TT])
        ones_bf = sb("ones_bf", [P, 1], BF16)

        k_flat = sb("k_flat", [ROWS + MROWS, SLOTS * GH * S2], BF16)
        k_aug = k_flat[:].rearrange("p (s h n) -> p s h n", s=SLOTS, h=GH)
        q_aug = sb("q_aug", [ROWS + MROWS, SLOTS, GH, T], BF16)
        v_aug = sb("v_aug", [P, KT, H, HD + 1])
        bias = sb("bias", [P, TT, S2], BF16)
        probs = sb("probs", [P, PRING, T])
        oT_sb = sb("oT_sb", [P, NG, T])
        x1_sb = sb("x1_sb", [P, TT, D])
        any_masked = sb("any_masked", [1, 1], I32)

        bias_next = sb("bias_next", [P, TT, S2], BF16)
        v_next = sb("v_next", [P, KT, D])
        x1_next = sb("x1_next", [P, TT, D])
        ctx_sb = sb("ctx_sb", [P, DC, S2])
        mask_sb = sb("mask_sb", [P, S2], I32)
        xT_sb = sb("xT_sb", [P, DC, T])
        x1T_sb = xT_sb
        x_sb = x1_next
        qk_sb = sb("qk_sb", [P, 2 * DC, T])
        v_sb = sb("v_sb", [P, TT, D])
        st_sb = sb("st_sb", [P, TT, 2 * P])
        parts = sb("parts", [P, 3, SRING, 512], BF16)
        rest = st_sb[:].rearrange("p t d -> p (t d)").rearrange("p (s n) -> p s n", s=2)
        u_sb = qk_sb[:, 2:4, :].rearrange("p a b -> p (a b)").rearrange("p (t d) -> p t d", t=TT)
        on_sb = v_sb
        onT_sb = st_sb[:].rearrange("p t d -> p (t d)").rearrange("p (c q) -> p c q", c=DC)
        x2_sb = qk_sb[:, 0:2, :].rearrange("p a b -> p (a b)").rearrange("p (t d) -> p t d", t=TT)

        stats = sb("stats", [P, TT, 6])
        mv = sb("mv", [P, TT, 2])
        ve = sb("ve", [P, TT])
        rstd = sb("rstd", [P, TT])
        mx = sb("mx", [P, 4, TT * GH])
        m_two = sb("m_two", [P, 2, TT * GH])
        m_full = sb("m_full", [P, TT * GH])
        m_rest = sb("m_rest", [P, TT * GH])
        m_parts = sb("m_parts", [P, TT * GH, MROWS], BF16)
        rsum = sb("rsum", [P, TT, H])
        lowest_sum = sb("lowest_sum", [1, 1])

        once = semaphores(ctx, nc, "s_weights s_ident0 s_ident s_const s_ones s_x2_out")
        s_weights, s_ident0, s_ident, s_const, s_ones, s_x2_out = once.values()

        per_batch = semaphores(
            ctx, nc,
            "s_x s_ctx s_mask s_bias s_step s_qk_sb s_v_sb s_band_sb s_u s_rest s_first s_second s_third "
            "s_var s_rstd s_normed s_summed s_x1 s_x1T_sb s_vx_sb s_flag s_dve s_store0 s_store1 s_store2 s_kl0 s_kl1 s_kl2 "
            "s_max s_max_taken s_mp s_mT s_mr s_st s_exp s_pv s_oTs "
            "s_tr s_on s_tr2 s_onT s_y s_residual s_x2 s_next")
        S = per_batch
        s_store = [S["s_store0"], S["s_store1"], S["s_store2"]]
        s_kl = [S["s_kl0"], S["s_kl1"], S["s_kl2"]]

        class Link:
            def __init__(self, dve):
                self.dve, self.n = dve, 0

            def __call__(self, ins):
                self.n += 1
                ins.then_inc(S["s_dve"], 1)
                self.dve.wait_ge(S["s_dve"], self.n)

        def norm_stats(link, dve, src):
            for t in range(TT):
                nc.vector.bn_stats(stats[:, t, :], src[:, t, :]).then_inc(S["s_dve"], 1)
                link.n += 1
            dve.wait_ge(S["s_dve"], link.n)
            for t in range(TT):
                nc.vector.bn_aggr(mv[:, t, :], stats[:, t, :]).then_inc(S["s_dve"], 1)
                link.n += 1
            dve.wait_ge(S["s_dve"], link.n)
            nc.vector.tensor_scalar(ve[:], mv[:, :, 1], EPS, None, ALU.add).then_inc(S["s_var"], 1)

        def norm_apply(link, dve, count, src, dst):
            dve.wait_ge(S["s_rstd"], count)
            for t in range(TT):
                nc.vector.tensor_scalar(dst[:, t, :], src[:, t, :], mv[:, t, 0:1], rstd[:, t:t + 1],
                                        ALU.subtract, ALU.mult).then_inc(S["s_dve"], 1)
                link.n += 1
            dve.wait_ge(S["s_dve"], link.n)

        def rsqrt(pool, n):
            pool.wait_ge(S["s_var"], n + 1)
            nc.gpsimd.tensor_tensor(rstd[:], ve[:], power[:], ALU.pow).then_inc(S["s_rstd"], 1)

        def pool_residual(pool):
            pool.wait_ge(S["s_normed"], 1)
            nc.gpsimd.tensor_tensor(u_sb[:], u_sb[:], bcast_rows(lnw_sb[:], TT), ALU.mult).then_inc(S["s_summed"], 1)
            pool.wait_ge(S["s_summed"], 1)
            nc.gpsimd.tensor_tensor(u_sb[:], u_sb[:], bcast_rows(lnb_sb[:], TT), ALU.add).then_inc(S["s_summed"], 1)
            pool.wait_ge(S["s_summed"], 2)
            nc.gpsimd.tensor_tensor(u_sb[:], u_sb[:], x_sb[:], ALU.add).then_inc(S["s_summed"], 1)

        def bcast_rows(ap, n):
            return ap.rearrange("p (a d) -> p a d", a=1).to_broadcast([P, n, ap.shape[1]])

        def taken(n):
            kind, i = STEPS[n][:2]
            return {"qk": (S["s_qk_sb"], i + 1), "v": (S["s_v_sb"], i + 1), "band": (S["s_band_sb"], 2 * i + 2),
                    "o": (S["s_u"], i + 1), "piece": (S["s_rest"], i + 1), "x1T": (S["s_x1T_sb"], i + 1),
                    "vx": (S["s_vx_sb"], i + 1)}[kind]

        def pe_step(pe, n, banks):
            kind, i = STEPS[n][:2]
            bk = banks[n % len(banks)]
            if n >= len(banks):
                pe.wait_ge(*taken(n - len(banks)))
            if kind == "qk":
                if i == 0:
                    pe.wait_ge(S["s_x"], 32)
                for c in range(DC):
                    last = nc.tensor.matmul(ps[:, bk, :], w_qkv_sb[:, c, i * P:(i + 1) * P], xT_sb[:, c, :],
                                            start=(c == 0), stop=(c == DC - 1))
            elif kind == "v":
                for u in range(2):
                    t = 2 * i + u
                    for c in range(DC):
                        last = nc.tensor.matmul(ps[:, bk, u * D:(u + 1) * D], xT_sb[:, c, t * P:(t + 1) * P],
                                                w_qkv_sb[:, c, 2 * D:3 * D], start=(c == 0), stop=(c == DC - 1))
            elif kind == "band":
                pe.wait_ge(S["s_qk_sb"], 2 * DC)
                for u in range(2):
                    t = 2 * i + u
                    w = min(2 * P, T - t * P)
                    for c in range(DC):
                        last = nc.tensor.matmul(ps[:, bk, u * 2 * P:u * 2 * P + w], qk_sb[:, DC + c, t * P:(t + 1) * P],
                                                qk_sb[:, c, t * P:t * P + w], start=(c == 0), stop=(c == DC - 1))
            elif kind == "o":
                pe.wait_ge(S["s_v_sb"], 2)
                pe.wait_ge(S["s_band_sb"], TT)
                for u in range(2):
                    t = 2 * i + u
                    last = nc.tensor.matmul(ps[:, bk, u * D:(u + 1) * D], st_sb[:, t, 0:P], v_sb[:, t, :],
                                            start=True, stop=(t == 0))
                    if t:
                        last = nc.tensor.matmul(ps[:, bk, u * D:(u + 1) * D], st_sb[:, t - 1, P:2 * P], v_sb[:, t - 1, :],
                                                start=False, stop=True)
            elif kind == "piece":
                is_q, m, c0, w = STEPS[n][2:]
                if is_q:
                    pe.wait_ge(S["s_x1T_sb"], DC)
                else:
                    pe.wait_ge(S["s_ctx"], 16)
                weight, source = (wq_sb, x1T_sb) if is_q else (wk_sb, ctx_sb)
                for c in range(DC):
                    last = nc.tensor.matmul(ps[:, bk, 0:w], weight[:, c, m * P:(m + 1) * P], source[:, c, c0:c0 + w],
                                            start=(c == 0), stop=(c == DC - 1))
            elif kind == "x1T":
                pe.wait_ge(S["s_x1"], 1)
                for t in range(TT):
                    last = nc.tensor.transpose(ps[:, bk, t * P:(t + 1) * P], x1_next[:, t, i * P:(i + 1) * P], ident[:])
            elif kind == "vx":
                for k in range(2 * i, min(2 * i + 2, KT)):
                    for c in range(DC):
                        last = nc.tensor.matmul(ps[0:KW[k], bk, k % 2 * D:(k % 2 + 1) * D], ctx_sb[:, c, k * P:k * P + KW[k]],
                                                wv_sb[:, c, :], start=(c == 0), stop=(c == DC - 1))
            else:
                pe.wait_ge(S["s_bias"], TT)
                for t in range(TT):
                    for c0, w in MAX_CHUNKS:
                        last = nc.tensor.matmul(ps[0:1, bk, 0:w], ones_bf[:], bias_next[:, t, c0:c0 + w],
                                                start=(t == 0 and c0 == 0), stop=(t == TT - 1 and c0 + w == S2),
                                                skip_group_check=True)
            last.then_inc(S["s_step"], 1)

        def act_step(act, n, banks):
            kind, i = STEPS[n][:2]
            bk = banks[n % len(banks)]
            if kind in ("v", "band", "any"):
                return
            act.wait_ge(S["s_step"], n + 1)
            if kind == "qk":
                nc.scalar.activation(qk_sb[:, i, :], ps[:, bk, :], ACT.Identity, bias=qk_bias[:, i:i + 1]).then_inc(S["s_qk_sb"], 1)
            elif kind == "o":
                nc.scalar.copy(u_sb[:, 2 * i:2 * i + 2, :].rearrange("p t d -> p (t d)"), ps[:, bk, :]).then_inc(S["s_u"], 1)
            elif kind == "piece":
                w = STEPS[n][5]
                if i >= SRING:
                    act.wait_ge(s_store[i % SRING], 16 * 3 * (i // SRING))
                nc.scalar.copy(parts[:, 0, i % SRING, 0:w], ps[:, bk, 0:w]).then_inc(S["s_first"], 1)
            elif kind == "x1T":
                nc.scalar.copy(x1T_sb[:, i, :], ps[:, bk, :]).then_inc(S["s_x1T_sb"], 1)
            elif 2 * i + 1 < KT:
                nc.scalar.copy(v_next[:, 2 * i:2 * i + 2, :].rearrange("p t d -> p (t d)"), ps[:, bk, :]).then_inc(S["s_vx_sb"], 1)
            else:
                nc.scalar.copy(v_next[0:KW[2 * i], 2 * i, :], ps[0:KW[2 * i], bk, 0:D]).then_inc(S["s_vx_sb"], 1)

        def act_second(act, n):
            i, w = STEPS[n][1], STEPS[n][5]
            act.wait_ge(S["s_rest"], i + 1)
            nc.scalar.copy(parts[:, 1, i % SRING, 0:w], rest[:, i % 2, 0:w]).then_inc(S["s_second"], 1)

        def pool_third(pool, i):
            w = STEPS[PIECE_STEPS[i]][5]
            pool.wait_ge(S["s_second"], i + 1)
            nc.gpsimd.tensor_tensor(parts[:, 2, i % SRING, 0:w], rest[:, i % 2, 0:w],
                                    parts[:, 1, i % SRING, 0:w], ALU.subtract).then_inc(S["s_third"], 1)

        def pool_mask(pool, t):
            pool.wait_ge(S["s_mask"], 16 * (t + 1))
            nc.gpsimd.tensor_scalar(bias_next[:, t, :], mask_sb[:], 0.0, MASKED,
                                    ALU.is_equal, ALU.mult).then_inc(S["s_bias"], 1)

        def dve_step(dve, link, n, banks):
            kind, i = STEPS[n][:2]
            bk = banks[n % len(banks)]
            if kind == "v":
                dve.wait_ge(S["s_step"], n + 1)
                nc.vector.tensor_tensor(v_sb[:, 2 * i:2 * i + 2, :], ps[:, bk, :].rearrange("p (t d) -> p t d", d=D),
                                        bcast_rows(v_bias[:], 2), ALU.add).then_inc(S["s_v_sb"], 1)
            elif kind == "band":
                dve.wait_ge(S["s_step"], n + 1)
                for u in range(2):
                    t = 2 * i + u
                    w = min(2 * P, T - t * P)
                    nc.vector.tensor_tensor(st_sb[:, t, 0:w], ps[:, bk, u * 2 * P:u * 2 * P + w], band[:, 0:w],
                                            ALU.mult).then_inc(S["s_band_sb"], 1)
            elif kind == "piece":
                w = STEPS[n][5]
                dve.wait_ge(S["s_first"], i + 1)
                if i >= 2:
                    dve.wait_ge(S["s_third"], i - 1)
                nc.vector.tensor_tensor(rest[:, i % 2, 0:w], ps[:, bk, 0:w], parts[:, 0, i % SRING, 0:w],
                                        ALU.subtract).then_inc(S["s_rest"], 1)
            elif kind == "any":
                dve.wait_ge(S["s_step"], n + 1)
                link(nc.vector.tensor_reduce(lowest_sum[:], ps[0:1, bk, 0:MAX_CHUNKS[0][1]], AX.X, ALU.min))
                nc.vector.tensor_scalar(any_masked[:], lowest_sum[:], 0.0, None, ALU.is_lt).then_inc(S["s_flag"], 1)

        def dve_norms(dve, link, part):
            if part == 0:
                dve.wait_ge(S["s_u"], 2)
                norm_stats(link, dve, u_sb)
            elif part == 1:
                norm_apply(link, dve, 1, u_sb, u_sb)
                nc.vector.engine_nop().then_inc(S["s_normed"], 1)
            elif part == 2:
                dve.wait_ge(S["s_summed"], 3)
                norm_stats(link, dve, u_sb)
            else:
                norm_apply(link, dve, 2, u_sb, x1_next)
                nc.vector.engine_nop().then_inc(S["s_x1"], 1)

        def load_rows(sp, row, mask_row):
            sp.dma_start(xT_sb[:], xT[:, row].rearrange("(c p) t -> p c t", p=P)).then_inc(S["s_x"], 16)
            sp.dma_start(x_sb[:], x[row, :].rearrange("(t p) d -> p t d", p=P)).then_inc(S["s_x"], 16)
            load_mask(sp, mask_row, 0)

        def load_ctx(sp, row):
            sp.dma_start(ctx_sb[:], ctxT[row, :].rearrange("(c p) n -> p c n", p=P)).then_inc(S["s_ctx"], 16)

        def load_mask(sp, mask_row, t):
            if t:
                sp.wait_ge(S["s_bias"], t)
            sp.dma_start(mask_sb[:], mask[mask_row(t), :]).then_inc(S["s_mask"], 16)

        def store_piece(sp, i, batch):
            is_q, m, c0, w = STEPS[PIECE_STEPS[i]][2:]
            sp.wait_ge(S["s_third"], i + 1)
            for row, count, part in (Q_ROWS if is_q else K_ROWS):
                dst = (q_dram if is_q else k_dram)[batch].rearrange("a (i p) h n -> (a i) (p h) n", p=HD)
                src = parts[:, part:part + count, i % SRING, 0:w] if not is_q else \
                    parts[:, part:part + 1, i % SRING, 0:w].to_broadcast([P, count, w])
                sp.dma_start(dst[row:row + count, m * P:(m + 1) * P, c0:c0 + w].rearrange("i r n -> r i n"),
                             src).then_inc(s_store[i % SRING], 16)

        def stores_done(sp):
            for s in range(SRING):
                sp.wait_ge(s_store[s], 16 * 3 * len(range(s, PIECES, SRING)))

        def load_group(sp, g, slot, batch):
            for dst, src in ((k_aug, k_dram), (q_aug, q_dram)):
                sp.dma_start(dst[0:ROWS, slot, :, :], src[batch, :, g * GH:(g + 1) * GH, :].rearrange("a r h n -> (a r) h n")).then_inc(s_kl[slot], 16)

        def pe_max(pe, n, slot):
            part, j, t = n % 4, n // 4 % GH, n // 16 % TT
            if n >= MAX_BANKS:
                pe.wait_ge(S["s_max_taken"], n - MAX_BANKS + 1)
            if n % GROUP_CHUNKS == 0 and n:
                pe.wait_ge(S["s_mr"], n // GROUP_CHUNKS)
            c0, w = MAX_CHUNKS[part]
            nc.tensor.matmul(ps[:, n % MAX_BANKS, 0:w], q_aug[0:ROWS, slot, j, t * P:(t + 1) * P],
                             k_aug[0:ROWS, slot, j, c0:c0 + w], start=True, stop=True).then_inc(S["s_max"], 1)

        def dve_max(dve, n, terms):
            part, j, t = n % 4, n // 4 % GH, n // 16 % TT
            c0, w = MAX_CHUNKS[part]
            dve.wait_ge(S["s_max"], n + 1)
            nc.vector.tensor_tensor_reduce(
                out=ps[:, n % MAX_BANKS, 0:w], in0=ps[:, n % MAX_BANKS, 0:w], in1=terms[:, t, c0:c0 + w], scale=1.0, scalar=LOWEST,
                op0=ALU.add, op1=ALU.max, accum_out=mx[:, part, t * GH + j:t * GH + j + 1]).then_inc(S["s_max_taken"], 1)

        def dve_max_parts(dve, link, count):
            dve.wait_ge(S["s_max_taken"], count * GROUP_CHUNKS)
            if count > 1:
                dve.wait_ge(S["s_mT"], count - 1)
            link(nc.vector.tensor_tensor(m_two[:], mx[:, 0:2, :], mx[:, 2:4, :], ALU.max))
            link(nc.vector.tensor_tensor(m_full[:], m_two[:, 0, :], m_two[:, 1, :], ALU.max))
            link(nc.vector.tensor_scalar(m_parts[:, :, 0], m_full[:], -1.0, None, ALU.mult))
            link(nc.vector.scalar_tensor_tensor(out=m_rest[:], in0=m_full[:], scalar=-1.0, in1=m_parts[:, :, 0],
                                                op0=ALU.mult, op1=ALU.subtract))
            link(nc.vector.tensor_copy(m_parts[:, :, 1], m_rest[:]))
            nc.vector.tensor_tensor(m_parts[:, :, 2], m_rest[:], m_parts[:, :, 1], ALU.subtract).then_inc(S["s_mp"], 1)
            dve.wait_ge(S["s_mp"], count)

        max_rows = ps[ROWS:ROWS + MROWS, 0:2, :].rearrange("p a b -> p (a b)").bitcast(BF16)

        def pe_max_rows(pe, count):
            pe.wait_ge(S["s_mp"], count)
            for j in range(GH):
                for t in range(TT):
                    c0 = j * T + t * P
                    last = nc.tensor.transpose(max_rows[:, c0:c0 + P], m_parts[:, t * GH + j, :], ident_bf[:])
            last.then_inc(S["s_mT"], 1)

        def act_max_rows(act, count, slot):
            act.wait_ge(S["s_mT"], count)
            nc.scalar.copy(q_aug[ROWS:ROWS + MROWS, slot, :, :].rearrange("p a b -> p (a b)"), max_rows).then_inc(S["s_mr"], 1)

        def attend(batch, row, mask_row, ctx_row, next_batch, stored, following):
            score_banks = SCORE_BANKS + ([] if following else STEP_BANKS)
            groups_max = NG if following else NG - 1

            def chunk_range(g, k):
                first, last = MAX_SPAN[g]
                if g >= groups_max or not first <= k < last:
                    return range(0)
                a, z = (GROUP_CHUNKS * (k + d - first) // (last - first) for d in (0, 1))
                return range(g * GROUP_CHUNKS + a, g * GROUP_CHUNKS + z)

            with nc.Block(no_gpsimd_drain=True) as block:
                @block.sync
                def _(sp):
                    sp.wait_ge(s_x2_out, stored)
                    if following:
                        load_rows(sp, row, mask_row)
                        load_ctx(sp, ctx_row)
                        for t in range(1, TT - 1):
                            load_mask(sp, mask_row, t)

                    def group(g):
                        before = SLOT.index(SLOT[g])
                        sp.wait_ge(S["s_st"], GH * KT * (before + 1))
                        if before:
                            sp.wait_ge(S["s_max"], GROUP_CHUNKS * before)
                        load_group(sp, g % NG, SLOT[g], next_batch if g == NG else batch)

                    if following:
                        load_mask(sp, mask_row, TT - 1)
                        for i in range(4):
                            store_piece(sp, i, next_batch)
                    group(3)
                    if following:
                        for i in range(4, PIECES):
                            store_piece(sp, i, next_batch)
                        stores_done(sp)
                        group(4)

                @block.tensor
                def _(pe):
                    def score_tile(n, masked):
                        g, k, j = n // (KT * GH), n // GH % KT, n % GH
                        if n % (KT * GH) == 0 and g:
                            pe.wait_ge(S["s_mr"], g)
                        if n >= len(score_banks):
                            pe.wait_ge(S["s_exp"], n - len(score_banks) + 1)
                        bk, w = score_banks[n % len(score_banks)], KW[k]
                        for t in range(TT if masked else 0):
                            nc.tensor.matmul(ps[0:w, bk, t * P:(t + 1) * P], bias[:, t, k * P:k * P + w], ident_bf[:],
                                             start=(t == 0), stop=False, skip_group_check=True)
                        last = nc.tensor.matmul(ps[0:w, bk, :], k_aug[:, SLOT[g], j, k * P:k * P + w], q_aug[:, SLOT[g], j, :],
                                                start=not masked, stop=True, skip_group_check=masked)
                        last.then_inc(S["s_st"], 1)

                    def weigh(n):
                        g, k, j = n // (KT * GH), n // GH % KT, n % GH
                        if k == 0 and j == 0 and g:
                            pe.wait_ge(S["s_oTs"], g)
                        pe.wait_ge(S["s_exp"], n + 1)
                        nc.tensor.matmul(ps[32 * j:32 * j + HD + 1, OUT_BANK, :], v_aug[0:KW[k], k, g * GH + j, :],
                                         probs[0:KW[k], n % PRING, :], start=(k == 0), stop=(k == KT - 1)).then_inc(S["s_pv"], 1)

                    def groups(masked):
                        done = 0
                        for g in range(NG):
                            for k in range(KT):
                                i = g * KT + k
                                chunks = list(chunk_range(g, k))
                                if chunks and k == MAX_SPAN[g][0] and g >= 2:
                                    pe.wait_ge(s_kl[SLOT[g + 1]], 32)
                                for j in range(GH):
                                    upto = min(i * GH + j + len(score_banks), NG * KT * GH)
                                    while done < upto:
                                        score_tile(done, masked)
                                        done += 1
                                    for n in chunks[len(chunks) * j // GH:len(chunks) * (j + 1) // GH]:
                                        pe_max(pe, n, SLOT[g + 1])
                                    if i * GH + j >= WEIGH_LAG:
                                        weigh(i * GH + j - WEIGH_LAG)
                                if g < groups_max and k == MAX_SPAN[g][1]:
                                    pe_max_rows(pe, g + 1)
                                for n in STEPS_AT.get(i, ()) if following else ():
                                    pe_step(pe, n, STEP_BANKS)
                        for n in range(NG * KT * GH - WEIGH_LAG, NG * KT * GH):
                            weigh(n)
                        if following:
                            pe_max_rows(pe, NG)

                    flag = pe.value_load(any_masked[0:1, 0:1], min_val=0, max_val=1)
                    with pe.If(flag > 0):
                        groups(masked=True)
                    with pe.Else():
                        groups(masked=False)

                @block.scalar
                def _(act):
                    def take_outputs(g):
                        act.wait_ge(S["s_pv"], (g + 1) * KT * GH)
                        nc.scalar.copy(oT_sb[:, g, :], ps[:, OUT_BANK, :]).then_inc(S["s_oTs"], 1)

                    for g in range(NG):
                        for k in range(KT):
                            i = g * KT + k
                            if g < NG - 1 and k == MAX_SPAN[g][1] + 1:
                                act_max_rows(act, g + 1, SLOT[g + 1])
                            for j in range(GH):
                                n = i * GH + j
                                act.wait_ge(S["s_st"], n + 1)
                                if n >= PRING:
                                    act.wait_ge(S["s_pv"], n - PRING + 1)
                                nc.scalar.activation(probs[0:KW[k], n % PRING, :], ps[0:KW[k], score_banks[n % len(score_banks)], :], ACT.Exp,
                                                     scale=HD ** -0.5).then_inc(S["s_exp"], 1)
                            if k == 0 and g:
                                take_outputs(g - 1)
                            if following:
                                for n in STEPS_AT.get(i - 1, ()):
                                    act_step(act, n, STEP_BANKS)
                                for n in STEPS_AT.get(i - 3, ()):
                                    if STEPS[n][0] == "piece":
                                        act_second(act, n)
                    take_outputs(NG - 1)
                    if following:
                        act_max_rows(act, NG, 0)

                @block.gpsimd
                def _(pool):
                    if following:
                        for t in range(TT - 1):
                            pool_mask(pool, t)
                        rsqrt(pool, 0)
                        pool_residual(pool)
                        pool_third(pool, 0)
                        rsqrt(pool, 1)
                        for i in range(1, 4):
                            pool_third(pool, i)
                        pool_mask(pool, TT - 1)
                        for i in range(4, PIECES):
                            pool_third(pool, i)

                @block.vector
                def _(dve):
                    link = Link(dve)
                    for g in range(NG):
                        for k in range(KT):
                            i = g * KT + k
                            for n in chunk_range(g, k):
                                if g == NG - 1 and n % GROUP_CHUNKS == 0:
                                    dve.wait_ge(S["s_bias"], TT)
                                dve_max(dve, n, bias if g < NG - 1 else bias_next)
                            if g < groups_max and k == MAX_SPAN[g][1] - 1:
                                dve_max_parts(dve, link, g + 1)
                            if following:
                                for lag, kinds in ((1, ("v", "band")), (2, ("piece",))):
                                    for n in STEPS_AT.get(i - lag, ()):
                                        if STEPS[n][0] in kinds:
                                            dve_step(dve, link, n, STEP_BANKS)
                                for part in NORMS_AT.get(i, ()):
                                    dve_norms(dve, link, part)
                    if following:
                        dve_step(dve, link, len(STEPS) - 1, STEP_BANKS)

        def hand_over(act):
            nc.scalar.copy(v_aug[:, 0:KT - 1, :, 0:HD], v_next[:, 0:KT - 1, :].rearrange("p k (h d) -> p k h d", h=H)).then_inc(S["s_next"], 1)
            nc.scalar.copy(v_aug[0:KW[-1], KT - 1, :, 0:HD],
                           v_next[0:KW[-1], KT - 1, :].rearrange("p (h d) -> p h d", h=H)).then_inc(S["s_next"], 1)

        def hand_over_residual(pool):
            nc.gpsimd.tensor_tensor(x1_sb[:], x1_next[:], bcast_rows(bo_sb[:], TT), ALU.add).then_inc(S["s_next"], 1)
            pool.wait_ge(S["s_next"], 4)

        def hand_over_bias():
            nc.vector.tensor_copy(bias[:].rearrange("p t n -> p (t n)"), bias_next[:].rearrange("p t n -> p (t n)")).then_inc(S["s_next"], 1)

        def project(row, next_batch, following):
            with nc.Block(no_gpsimd_drain=True) as block:
                @block.sync
                def _(sp):
                    if following:
                        load_group(sp, 1, 1, next_batch)
                        load_group(sp, 2, 2, next_batch)
                    sp.wait_ge(S["s_x2"], 1)
                    sp.dma_start(x2_dram[row, :].rearrange("(t p) d -> p t d", p=P), x2_sb).then_inc(s_x2_out, 16)
                    if following:
                        sp.wait_ge(s_kl[1], 32 * 2)
                        sp.wait_ge(s_kl[2], 32)
                    else:
                        sp.wait_ge(s_x2_out, 16 * (B + 1))

                @block.tensor
                def _(pe):
                    for t in range(TT):
                        for g in range(NG):
                            last = nc.tensor.transpose(ps[:, t, g * P:(g + 1) * P], oT_sb[:, g, t * P:(t + 1) * P], ident[:])
                        last.then_inc(S["s_tr"], 1)
                    for t in range(TT):
                        pe.wait_ge(S["s_on"], t + 1)
                        for c in range(DC):
                            last = nc.tensor.transpose(ps[:, 4 + t, c * P:(c + 1) * P], on_sb[:, t, c * P:(c + 1) * P], ident[:])
                        last.then_inc(S["s_tr2"], 1)
                    for t in range(TT):
                        pe.wait_ge(S["s_onT"], t + 1)
                        for c in range(DC):
                            last = nc.tensor.matmul(ps[:, t, 0:D], onT_sb[:, c, t * P:(t + 1) * P], wo_sb[:, c, :],
                                                    start=(c == 0), stop=(c == DC - 1))
                        last.then_inc(S["s_y"], 1)

                @block.scalar
                def _(act):
                    if following:
                        hand_over(act)
                    for t in range(TT):
                        act.wait_ge(S["s_tr2"], t + 1)
                        nc.scalar.copy(onT_sb[:, :, t * P:(t + 1) * P],
                                       ps[:, 4 + t, 0:D].rearrange("p (c q) -> p c q", c=DC)).then_inc(S["s_onT"], 1)

                @block.gpsimd
                def _(pool):
                    rsqrt(pool, 2 if following else 0)
                    if following:
                        pool.wait_ge(S["s_residual"], TT)
                        hand_over_residual(pool)

                @block.vector
                def _(dve):
                    link = Link(dve)
                    link.n = DVE_ATTEND + (DVE_PREPARE if following else -5)
                    if following:
                        hand_over_bias()
                    for t in range(TT):
                        dve.wait_ge(S["s_tr"], t + 1)
                        heads = ps[:, t, :].rearrange("p (h d) -> p h d", h=H)
                        link(nc.vector.reciprocal(rsum[:, t, :], heads[:, :, HD]))
                        nc.vector.tensor_tensor(on_sb[:, t, :].rearrange("p (h d) -> p h d", h=H), heads[:, :, 0:HD],
                                                rsum[:, t, :].rearrange("p (h a) -> p h a", a=1).to_broadcast([P, H, HD]),
                                                ALU.mult).then_inc(S["s_on"], 1)
                    for t in range(TT):
                        dve.wait_ge(S["s_y"], t + 1)
                        nc.vector.tensor_tensor(u_sb[:, t, :], ps[:, t, 0:D], x1_sb[:, t, :], ALU.add).then_inc(S["s_residual"], 1)
                    dve.wait_ge(S["s_residual"], TT)
                    norm_stats(link, dve, u_sb)
                    norm_apply(link, dve, 3 if following else 1, u_sb, x2_sb)
                    nc.vector.engine_nop().then_inc(S["s_x2"], 1)

        with nc.Block(no_gpsimd_drain=True) as block:
            @block.sync
            def _(sp):
                load_rows(sp, slice(0, T), lambda t: slice(t * P, (t + 1) * P))
                for dst, src in ((w_qkv_sb, w_qkv), (wk_sb, wkT), (wq_sb, wqT), (wv_sb, wvT), (wo_sb, woT)):
                    sp.dma_start(dst[:], src.rearrange("(c p) n -> p c n", p=P)).then_inc(s_weights, 16)
                with nc.allow_non_contiguous_dma(reason="512 bias values, once"):
                    sp.dma_start(qk_bias[:], b_qkv[0:2 * D].rearrange("(c p) -> p c", p=P)).then_inc(s_weights, 16)
                for dst, src in ((v_bias, b_qkv[2 * D:3 * D]), (lnw_sb, ln_w), (lnb_sb, ln_b), (bo_sb, bo)):
                    sp.dma_start(dst[:], src.rearrange("(a n) -> a n", a=1).to_broadcast([P, D])).then_inc(s_weights, 16)
                load_ctx(sp, slice(0, D))
                sp.sem_inc(s_x2_out, 16)
                sp.wait_ge(s_weights, 16 * 10)

            @block.gpsimd
            def _(pool):
                nc.gpsimd.memset(ident[:], 0.0).then_inc(s_ident0, 1)
                nc.gpsimd.memset(band[:], 1.0 / (D * SPAN) ** 0.5).then_inc(s_ident0, 1)
                nc.gpsimd.memset(power[:], -0.5).then_inc(s_ident0, 1)
                pool.wait_ge(s_ident0, 2)
                nc.gpsimd.affine_select(out=ident[:], in_=ident[:], compare_op=ALU.not_equal, fill=1.0,
                                        base=0, pattern=[[-1, P]], channel_multiplier=1).then_inc(s_ident, 1)
                nc.gpsimd.affine_select(out=band[:], in_=band[:], compare_op=ALU.is_ge, fill=0.0,
                                        base=0, pattern=[[1, 2 * P]], channel_multiplier=-1).then_inc(s_const, 1)
                pool.wait_ge(s_const, 1)
                nc.gpsimd.affine_select(out=band[:], in_=band[:], compare_op=ALU.is_ge, fill=0.0,
                                        base=SPAN - 1, pattern=[[-1, 2 * P]], channel_multiplier=1).then_inc(s_const, 1)
                pool.wait_ge(s_const, 2)

            @block.vector
            def _(dve):
                nc.vector.memset(v_aug[:, :, :, HD:HD + 1], 1.0).then_inc(s_ones, 1)
                nc.vector.memset(k_flat[ROWS:ROWS + MROWS, :].bitcast(F32), TWO_ONES).then_inc(s_ones, 1)
                dve.wait_ge(s_ident, 1)
                nc.vector.tensor_copy(ident_bf[:], ident[:]).then_inc(s_ones, 1)
                nc.vector.memset(ones_bf[:], 1.0).then_inc(s_ones, 1)
                nc.vector.memset(ps[:, OUT_BANK, :], 0.0).then_inc(s_ones, 1)
                dve.wait_ge(s_ones, 5)

        with nc.Block(no_gpsimd_drain=True) as block:
            @block.sync
            def _(sp):
                def mask_row(t):
                    return slice(t * P, (t + 1) * P)

                load_mask(sp, mask_row, 1)
                for i in range(6):
                    store_piece(sp, i, slice(0, 1))
                load_mask(sp, mask_row, 2)
                for i in range(6, PIECES):
                    store_piece(sp, i, slice(0, 1))
                stores_done(sp)
                for g in range(SLOTS):
                    load_group(sp, g, g, slice(0, 1))
                load_mask(sp, mask_row, 3)
                for slot in range(SLOTS):
                    sp.wait_ge(s_kl[slot], 32)

            @block.tensor
            def _(pe):
                for n in range(len(STEPS) - 1):
                    pe_step(pe, n, FIRST_BANKS)
                pe.wait_ge(s_kl[0], 32)
                for n in range(GROUP_CHUNKS):
                    pe_max(pe, n, 0)
                pe_max_rows(pe, 1)
                pe_step(pe, len(STEPS) - 1, FIRST_BANKS)

            @block.scalar
            def _(act):
                for n in range(len(STEPS)):
                    act_step(act, n, FIRST_BANKS)
                    if n and STEPS[n - 1][0] == "piece":
                        act_second(act, n - 1)
                act.wait_ge(S["s_vx_sb"], -(-KT // 2))
                hand_over(act)
                act_max_rows(act, 1, 0)

            @block.gpsimd
            def _(pool):
                pool_mask(pool, 0)
                rsqrt(pool, 0)
                pool_residual(pool)
                rsqrt(pool, 1)
                for i in range(4):
                    pool_third(pool, i)
                pool_mask(pool, 1)
                for i in range(4, PIECES):
                    pool_third(pool, i)
                pool_mask(pool, 2)
                pool_mask(pool, 3)
                hand_over_residual(pool)

            @block.vector
            def _(dve):
                link = Link(dve)
                for n in range(len(STEPS) - 1):
                    dve_step(dve, link, n, FIRST_BANKS)
                    if STEPS[n][:2] == ("o", 1):
                        for part in range(NORM_PARTS):
                            dve_norms(dve, link, part)
                for n in range(GROUP_CHUNKS):
                    if n % 16 == 0:
                        dve.wait_ge(S["s_bias"], n // 16 + 1)
                    dve_max(dve, n, bias_next)
                dve_max_parts(dve, link, 1)
                dve_step(dve, link, len(STEPS) - 1, FIRST_BANKS)
                hand_over_bias()

        nc.all_engine_barrier(sems_to_clear=as_range(per_batch.values()))

        with nc.Fori(0, B - 1) as b:
            attend(bass.ds(b, 1), bass.ds(b * T + T, T), lambda t: bass.ds(b * T + (T + t * P), P),
                   bass.ds(b * D + D, D), bass.ds(b + 1, 1), b * 16 + 16, following=True)
            project(bass.ds(b * T, T), bass.ds(b + 1, 1), following=True)
            nc.all_engine_barrier(sems_to_clear=as_range(per_batch.values()))
        attend(slice(B - 1, B), None, None, None, None, 16 * B, following=False)
        project(slice((B - 1) * T, B * T), None, following=False)


DVE_NORM = 3 * TT
DVE_PREPARE = 2 * DVE_NORM + 1
DVE_ATTEND = 5 * NG


def mixture(nc, x2_dram, ident, ps, router_wT, correction, up_w, down_w, out):
    with ExitStack() as ctx:
        def sb(name, shape, dt=F32):
            return ctx.enter_context(nc.sbuf_tensor(name, shape, dt))

        x2 = sb("x2", [P, NT, D])
        x2T = sb("x2T", [P, 2, DC, NT * P], F32R)
        router_sb = sb("router_sb", [P, DC, E])
        router_hl = sb("router_hl", [P, 2, DC, E], F32R)
        corr_sb = sb("corr_sb", [P, E])
        lower = sb("lower", [P, G, G])
        power = sb("power_m", [P, NT])
        scores = sb("scores", [P, NT, E])
        sfc = sb("sfc", [P, NT, E])
        work = sb("work", [P, NT, E])
        work2 = sb("work2", [P, NT, E])
        m1 = sb("m1", [P, NT * G])
        m2 = sb("m2", [P, NT * G])
        cnt = sb("cnt", [P, NT * G])
        top8 = sb("top8", [P, NT, K_TOP])
        total = sb("total", [P, NT])
        logitT = sb("logitT", [E, NT * P])
        combine = sb("combine", [P, NT, EXPERTS])
        w_in = sb("w_in", [P, 2, 2 * D])
        w_hl = sb("w_hl", [P, 2, 2, 2 * D], F32R)
        hr = sb("hr", [P, 4, 512])
        hs = sb("hs", [P, 4, 512])
        h2 = sb("h2", [P, 2, 2, NT * P], F32R)
        result = sb("result", [P, NT, D])
        stats = sb("stats_m", [P, NT, 6])
        mv = sb("mv_m", [P, NT, 2])
        ve = sb("ve_m", [P, NT])
        rstd = sb("rstd_m", [P, NT])

        S = semaphores(ctx, nc, "r_x0 r_x1 r_x2 r_x3 r_load r_const0 r_const r_router r_xT r_xTs r_xTl r_logitT r_logitTs r_logit r_exp r_dve "
                                "s_wu0 s_wu1 s_wd0 s_wd1 s_up_hi s_up_lo s_down_hi s_down_lo s_up s_relu s_square s_h_hi s_h_lo "
                                "s_y2 s_y_free s_var2 s_rstd2 s_final s_store")

        def route_sync(sp):
            for q in range(B):
                sp.dma_start(x2[:, q * TT:(q + 1) * TT, :],
                             x2_dram[q * T:(q + 1) * T, :].rearrange("(t p) d -> p t d", p=P)).then_inc(S[f"r_x{q}"], 16)
            sp.dma_start(router_sb[:], router_wT.rearrange("(c p) n -> p c n", p=P)).then_inc(S["r_load"], 16)
            sp.dma_start(corr_sb[:], correction.rearrange("(a n) -> a n", a=1).to_broadcast([P, E])).then_inc(S["r_load"], 16)

        def route_gpsimd(pool):
            nc.gpsimd.memset(lower[:], 1.0).then_inc(S["r_const0"], 1)
            nc.gpsimd.memset(power[:], -0.5).then_inc(S["r_const0"], 1)
            nc.gpsimd.memset(combine[:], 1.0).then_inc(S["r_const0"], 1)
            pool.wait_ge(S["r_const0"], 3)
            nc.gpsimd.affine_select(out=lower[:], in_=lower[:], compare_op=ALU.is_gt, fill=0.0,
                                    base=0, pattern=[[1, G], [-1, G]], channel_multiplier=0).then_inc(S["r_const"], 1)

        def route_tensor(pe):
            for t in range(NT):
                if t % TT == 0:
                    pe.wait_ge(S[f"r_x{t // TT}"], 16)
                if t >= 4:
                    pe.wait_ge(S["r_xTl"], t - 3)
                for c in range(DC):
                    last = nc.tensor.transpose(ps[:, 4 + t % 4, c * P:(c + 1) * P], x2[:, t, c * P:(c + 1) * P], ident[:])
                last.then_inc(S["r_xT"], 1)
            pe.wait_ge(S["r_load"], 32)
            pe.wait_ge(S["r_router"], 2)
            for q in range(4):
                pe.wait_ge(S["r_xTl"], 4 * q + 4)
                for n, (a, w, c) in enumerate(PASSES):
                    last = nc.tensor.matmul(ps[0:E, q, :], router_hl[:, w, c, :], x2T[:, a, c, q * 512:(q + 1) * 512],
                                            start=(n == 0), stop=(n == len(PASSES) - 1))
                last.then_inc(S["r_logitT"], 1)
            pe.wait_ge(S["r_xTl"], NT)
            for q in range(4):
                pe.wait_ge(S["r_logitTs"], q + 1)
                for t in range(4 * q, 4 * q + 4):
                    last = nc.tensor.transpose(ps[:, 4 + t // 8, (t % 8) * E:(t % 8 + 1) * E],
                                               logitT[:, t * P:(t + 1) * P], ident[0:E, 0:E])
            last.then_inc(S["r_logit"], 1)

        def route_scalar(act):
            for t in range(NT):
                act.wait_ge(S["r_xT"], t + 1)
                nc.scalar.copy(x2T[:, 0, :, t * P:(t + 1) * P],
                               ps[:, 4 + t % 4, 0:D].rearrange("p (c q) -> p c q", c=DC)).then_inc(S["r_xTs"], 1)
            for q in range(4):
                act.wait_ge(S["r_logitT"], q + 1)
                nc.scalar.copy(logitT[:, q * 512:(q + 1) * 512], ps[0:E, q, :]).then_inc(S["r_logitTs"], 1)
            act.wait_ge(S["r_logit"], 1)
            nc.scalar.activation(work[:].rearrange("p t e -> p (t e)"), ps[:, 4:6, :].rearrange("p a b -> p (a b)"),
                                 ACT.Exp, scale=-1.0).then_inc(S["r_exp"], 1)

        def route_vector(dve):
            n = [0]

            def link(ins):
                n[0] += 1
                ins.then_inc(S["r_dve"], 1)
                dve.wait_ge(S["r_dve"], n[0])

            def by_group(ap):
                return ap[:].rearrange("p t (g e) -> p (t g) e", g=G)

            def over(ap, k):
                return ap.rearrange("p (n a) -> p n a", a=1).to_broadcast([P, ap.shape[1], k])

            dve.wait_ge(S["r_load"], 32)
            nc.vector.tensor_copy(router_hl[:, 0, :, :], router_sb[:]).then_inc(S["r_router"], 1)
            dve.wait_ge(S["r_router"], 1)
            nc.vector.tensor_tensor(router_hl[:, 1, :, :], router_sb[:], router_hl[:, 0, :, :].bitcast(F32),
                                    ALU.subtract).then_inc(S["r_router"], 1)
            for t in range(NT):
                dve.wait_ge(S["r_xTs"], t + 1)
                nc.vector.tensor_tensor(x2T[:, 1, :, t * P:(t + 1) * P],
                                        ps[:, 4 + t % 4, 0:D].rearrange("p (c q) -> p c q", c=DC),
                                        x2T[:, 0, :, t * P:(t + 1) * P].bitcast(F32), ALU.subtract).then_inc(S["r_xTl"], 1)
            dve.wait_ge(S["r_exp"], 1)
            link(nc.vector.tensor_scalar(work[:], work[:], 1.0, None, ALU.add))
            link(nc.vector.reciprocal(scores[:], work[:]))
            link(nc.vector.tensor_tensor(sfc[:], scores[:], corr_sb[:].rearrange("p (a e) -> p a e", a=1).to_broadcast([P, NT, E]), ALU.add))
            link(nc.vector.tensor_reduce(m1[:], by_group(sfc), AX.X, ALU.max))
            link(nc.vector.tensor_tensor(by_group(work), by_group(sfc), over(m1[:], E // G), ALU.is_equal))
            link(nc.vector.tensor_reduce(cnt[:], by_group(work), AX.X, ALU.add))
            link(nc.vector.scalar_tensor_tensor(out=work2[:], in0=work[:], scalar=LOWEST, in1=sfc[:], op0=ALU.mult, op1=ALU.add))
            link(nc.vector.tensor_reduce(m2[:], by_group(work2), AX.X, ALU.max))
            link(nc.vector.tensor_scalar(cnt[:], cnt[:], 1.5, 1.0, ALU.is_gt, ALU.subtract))
            link(nc.vector.scalar_tensor_tensor(out=cnt[:], in0=cnt[:], scalar=-LOWEST, in1=m1[:], op0=ALU.mult, op1=ALU.add))
            link(nc.vector.tensor_tensor(m2[:], m2[:], cnt[:], ALU.max))
            link(nc.vector.tensor_tensor(m1[:], m1[:], m2[:], ALU.add))
            others = m1[:].rearrange("p (t a g) -> p t a g", a=1, g=G).to_broadcast([P, NT, G, G])
            itself = m1[:].rearrange("p (t g a) -> p t g a", a=1, g=G).to_broadcast([P, NT, G, G])
            w4 = work[:].rearrange("p t (g e) -> p t g e", g=G)
            v4 = work2[:].rearrange("p t (g e) -> p t g e", g=G)
            dve.wait_ge(S["r_const"], 1)
            link(nc.vector.tensor_tensor(w4, others, itself, ALU.is_gt))
            link(nc.vector.tensor_tensor(v4, others, itself, ALU.is_equal))
            link(nc.vector.tensor_tensor(v4, v4, lower[:].rearrange("p (a g) e -> p a g e", a=1).to_broadcast([P, NT, G, G]), ALU.mult))
            link(nc.vector.tensor_tensor(work[:], work[:], work2[:], ALU.add))
            link(nc.vector.tensor_reduce(cnt[:], by_group(work), AX.X, ALU.add))
            link(nc.vector.tensor_scalar(cnt[:], cnt[:], TOPK_GROUP - 0.5, None, ALU.is_lt))
            link(nc.vector.tensor_tensor(by_group(work), by_group(sfc), over(cnt[:], E // G), ALU.mult))
            for t in range(NT):
                n[0] += 1
                nc.vector.max(top8[:, t, :], work[:, t, :]).then_inc(S["r_dve"], 1)
            dve.wait_ge(S["r_dve"], n[0])
            for t in range(NT):
                n[0] += 1
                nc.vector.match_replace(work2[:, t, :], top8[:, t, :], work[:, t, :], LOWEST).then_inc(S["r_dve"], 1)
            dve.wait_ge(S["r_dve"], n[0])
            link(nc.vector.tensor_scalar(work2[:], work2[:], LOWEST / 2, None, ALU.is_lt))
            link(nc.vector.tensor_tensor(work2[:], work2[:], scores[:], ALU.mult))
            link(nc.vector.tensor_reduce(total[:], work2[:], AX.X, ALU.add))
            link(nc.vector.tensor_scalar(total[:], total[:], 1e-20, None, ALU.add))
            link(nc.vector.reciprocal(total[:], total[:]))
            link(nc.vector.tensor_tensor(work2[:], work2[:], over(total[:], E), ALU.mult))
            link(nc.vector.tensor_scalar(combine[:, :, 0:E], work2[:], ROUTE_SCALE, None, ALU.mult))

        PAIRS = NT // 2
        up_v = up_w.rearrange("e (c p) i -> p e c i", p=P)
        down_v = down_w.rearrange("e i d -> i e d")
        s_wu, s_wd = [S["s_wu0"], S["s_wu1"]], [S["s_wd0"], S["s_wd1"]]
        LOOPS = EXPERTS // 2

        with nc.Block(no_gpsimd_drain=True) as block:
            @block.sync
            def _(sp):
                def load_up(k, s):
                    sp.dma_start(w_in[:, s:s + 1, 0:D].rearrange("p s (c i) -> p s c i", c=DC), up_v[:, k, :, :]).then_inc(s_wu[s], 16)

                def load_down(k, s):
                    sp.dma_start(w_in[:, s:s + 1, D:2 * D], down_v[:, k, :]).then_inc(s_wd[s], 16)

                route_sync(sp)
                for s in range(2):
                    load_up(slice(s, s + 1), s)
                    load_down(slice(s, s + 1), s)
                with sp.Fori(1, LOOPS) as i:
                    for s in range(2):
                        sp.wait_ge(S["s_up_lo"], i * 2 + (s - 1))
                        load_up(bass.ds(i * 2 + s, 1), s)
                        sp.wait_ge(S["s_down_lo"], i * 2 + (s - 1))
                        load_down(bass.ds(i * 2 + s, 1), s)
                out_v = out.rearrange("(t p) d -> p t d", p=P)
                for q in range(4):
                    sp.wait_ge(S["s_final"], 4 * q + 4)
                    sp.dma_start(out_v[:, 4 * q:4 * q + 4, :], result[:, 4 * q:4 * q + 4, :]).then_inc(S["s_store"], 16)
                sp.wait_ge(S["s_store"], 64)

            @block.tensor
            def _(pe):
                def up(k, s, first=False):
                    pe.wait_ge(S["s_up_lo"], k + 1)
                    for q in range(4):
                        if not first:
                            pe.wait_ge(S["s_relu"], k * 4 + (q - 3))
                        for n, (a, w, c) in enumerate(PASSES):
                            last = nc.tensor.matmul(ps[:, q, :], w_hl[:, s, w, c * I_MOE:(c + 1) * I_MOE],
                                                    x2T[:, a, c, q * 512:(q + 1) * 512],
                                                    start=(n == 0), stop=(n == len(PASSES) - 1))
                        last.then_inc(S["s_up"], 1)

                def down(k, s):
                    pe.wait_ge(S["s_down_lo"], k + 1)
                    for r in range(PAIRS):
                        if r % 2 == 0:
                            pe.wait_ge(S["s_h_lo"], k * 4 + (r // 2 + 1))
                        pe.wait_ge(S["s_y_free"], k * PAIRS + (r + 1))
                        for u in range(2):
                            t = 2 * r + u
                            for n, (a, w) in enumerate(((0, 0), (0, 1), (1, 0))):
                                last = nc.tensor.matmul(ps[:, 4 + r % 4, u * D:(u + 1) * D], h2[:, s, a, t * P:(t + 1) * P],
                                                        w_hl[:, s, w, D:2 * D], start=(n == 0), stop=(n == 2))
                        last.then_inc(S["s_y2"], 1)

                route_tensor(pe)
                pe.wait_ge(S["r_exp"], 1)
                up(0, 0, first=True)
                with pe.Fori(0, LOOPS - 1) as i:
                    up(i * 2 + 1, 1)
                    down(i * 2, 0)
                    up(i * 2 + 2, 0)
                    down(i * 2 + 1, 1)
                up(EXPERTS - 1, 1)
                down(EXPERTS - 2, 0)
                down(EXPERTS - 1, 1)

            @block.scalar
            def _(act):
                def up_high(k, s, load, first=False):
                    act.wait_ge(s_wu[s], load * 16)
                    if not first:
                        act.wait_ge(S["s_up"], k * 4 - 4)
                    nc.scalar.copy(w_hl[:, s, 0, 0:D], w_in[:, s, 0:D]).then_inc(S["s_up_hi"], 1)

                def relu(k, q, first):
                    if not (first and k == 0):
                        act.wait_ge(S["s_square"], k * 4 + (q - 3))
                    act.wait_ge(S["s_up"], k * 4 + (q + 1))
                    nc.scalar.activation(hr[:, q, :], ps[:, q, :], ACT.Relu).then_inc(S["s_relu"], 1)

                def high(k, s, q):
                    act.wait_ge(S["s_square"], k * 4 + (q + 1))
                    nc.scalar.copy(h2[:, s, 0, q * 512:(q + 1) * 512], hs[:, q, :]).then_inc(S["s_h_hi"], 1)

                def down_high(k, s, load, first):
                    act.wait_ge(s_wd[s], load * 16)
                    if not first:
                        act.wait_ge(S["s_y2"], k * PAIRS - PAIRS)
                    nc.scalar.copy(w_hl[:, s, 0, D:2 * D], w_in[:, s, D:2 * D]).then_inc(S["s_down_hi"], 1)

                def hidden(k, s, load, first=False):
                    relu(k, 0, first)
                    relu(k, 1, first)
                    high(k, s, 0)
                    relu(k, 2, first)
                    high(k, s, 1)
                    relu(k, 3, first)
                    high(k, s, 2)
                    down_high(k, s, load, first)
                    high(k, s, 3)

                route_scalar(act)
                up_high(0, 0, 1, first=True)
                up_high(1, 1, 1, first=True)
                hidden(0, 0, 1, first=True)
                up_high(2, 0, 2)
                hidden(1, 1, 1, first=True)
                with act.Fori(1, LOOPS - 1) as i:
                    up_high(i * 2 + 1, 1, i + 1)
                    hidden(i * 2, 0, i + 1)
                    up_high(i * 2 + 2, 0, i + 2)
                    hidden(i * 2 + 1, 1, i + 1)
                up_high(EXPERTS - 1, 1, LOOPS)
                hidden(EXPERTS - 2, 0, LOOPS)
                hidden(EXPERTS - 1, 1, LOOPS)

            @block.gpsimd
            def _(pool):
                def low(k, s, columns, s_high, s_low):
                    pool.wait_ge(s_high, k + 1)
                    nc.gpsimd.tensor_tensor(w_hl[:, s, 1, columns], w_in[:, s, columns], w_hl[:, s, 0, columns].bitcast(F32),
                                            ALU.subtract).then_inc(s_low, 1)

                def up_low(k, s):
                    low(k, s, slice(0, D), S["s_up_hi"], S["s_up_lo"])

                def square(k, s, first=False):
                    for q in range(4):
                        pool.wait_ge(S["s_relu"], k * 4 + (q + 1))
                        if not first:
                            pool.wait_ge(S["s_h_lo"], k * 4 + (q - 3))
                        nc.gpsimd.tensor_tensor(hs[:, q, :], hr[:, q, :], hr[:, q, :], ALU.mult).then_inc(S["s_square"], 1)
                    low(k, s, slice(D, 2 * D), S["s_down_hi"], S["s_down_lo"])

                route_gpsimd(pool)
                up_low(0, 0)
                up_low(1, 1)
                square(0, 0, first=True)
                with pool.Fori(1, LOOPS) as i:
                    up_low(i * 2, 0)
                    square(i * 2 - 1, 1)
                    up_low(i * 2 + 1, 1)
                    square(i * 2, 0)
                square(EXPERTS - 1, 1)
                pool.wait_ge(S["s_var2"], 1)
                nc.gpsimd.tensor_tensor(rstd[:], ve[:], power[:], ALU.pow).then_inc(S["s_rstd2"], 1)

            @block.vector
            def _(dve):
                dve.sem_inc(S["s_y_free"], 4)
                route_vector(dve)

                def low(k, s, q):
                    dve.wait_ge(S["s_h_hi"], k * 4 + (q + 1))
                    nc.vector.tensor_tensor(h2[:, s, 1, q * 512:(q + 1) * 512], hs[:, q, :],
                                            h2[:, s, 0, q * 512:(q + 1) * 512].bitcast(F32), ALU.subtract).then_inc(S["s_h_lo"], 1)

                def add(k, r):
                    dve.wait_ge(S["s_y2"], k * PAIRS + (r + 1))
                    for u in range(2):
                        t = 2 * r + u
                        last = nc.vector.scalar_tensor_tensor(
                            out=x2[:, t, :], in0=ps[:, 4 + r % 4, u * D:(u + 1) * D],
                            scalar=combine[:, t, k:k + 1] if isinstance(k, int) else combine[:, t, bass.ds(k, 1)],
                            in1=x2[:, t, :], op0=ALU.mult, op1=ALU.add)
                    last.then_inc(S["s_y_free"], 1)

                def step(k, s):
                    for r in range(PAIRS):
                        add(k, r)
                    for q in range(4):
                        low(k + 1, s, q)

                for q in range(4):
                    low(0, 0, q)
                with dve.Fori(0, LOOPS - 1) as i:
                    step(i * 2, 1)
                    step(i * 2 + 1, 0)
                step(EXPERTS - 2, 1)
                for r in range(PAIRS):
                    add(EXPERTS - 1, r)
                dve.wait_ge(S["s_y_free"], EXPERTS * PAIRS + 4)
                base = [DVE_ROUTE]

                def counted(ins):
                    base[0] += 1
                    ins.then_inc(S["r_dve"], 1)
                for t in range(NT):
                    counted(nc.vector.bn_stats(stats[:, t, :], x2[:, t, :]))
                dve.wait_ge(S["r_dve"], base[0])
                for t in range(NT):
                    counted(nc.vector.bn_aggr(mv[:, t, :], stats[:, t, :]))
                dve.wait_ge(S["r_dve"], base[0])
                nc.vector.tensor_scalar(ve[:], mv[:, :, 1], EPS, None, ALU.add).then_inc(S["s_var2"], 1)
                dve.wait_ge(S["s_rstd2"], 1)
                for t in range(NT):
                    nc.vector.tensor_scalar(result[:, t, :], x2[:, t, :], mv[:, t, 0:1], rstd[:, t:t + 1],
                                            ALU.subtract, ALU.mult).then_inc(S["s_final"], 1)


DVE_ROUTE = 19 + 2 * NT + 7


def kernel(x, ctx_1024, mask_Bx1xSxS2_if1, L0_attn_W_qkv, L0_attn_b_qkv, L0_attn_ln_w, L0_attn_ln_b,
           L0_xattn_Wq, L0_xattn_Wk, L0_xattn_Wv, L0_xattn_Wo, L0_xattn_bo, L0_ffn_router_w,
           L0_ffn_correction_bias, L0_ffn_up_w, L0_ffn_down_w, L0_ffn_shared_up_w, L0_ffn_shared_down_w):
    import numpy as np
    import concourse.bacc as bacc
    from concourse.bass_utils import run_bass_kernel_spmd

    x_rows = np.asarray(x).reshape(B * T, D)
    shared_up = np.asarray(L0_ffn_shared_up_w).reshape(D, EXPERTS - E, I_MOE).transpose(1, 0, 2)
    shared_down = np.asarray(L0_ffn_shared_down_w).reshape(EXPERTS - E, I_MOE, D)

    def by_width(w):
        return np.asarray(w).reshape(H, HD, D).transpose(2, 1, 0).reshape(D, D)

    given = {
        "x": x_rows, "xT": x_rows.T,
        "ctxT": np.asarray(ctx_1024).transpose(0, 2, 1).reshape(B * D, S2),
        "mask": np.asarray(mask_Bx1xSxS2_if1).reshape(B * T, S2),
        "w_qkv": L0_attn_W_qkv, "b_qkv": L0_attn_b_qkv, "ln_w": L0_attn_ln_w, "ln_b": L0_attn_ln_b,
        "wqT": by_width(L0_xattn_Wq), "wkT": by_width(L0_xattn_Wk),
        "wvT": np.asarray(L0_xattn_Wv).T, "woT": np.asarray(L0_xattn_Wo).T, "bo": L0_xattn_bo,
        "router_wT": np.asarray(L0_ffn_router_w).T, "correction": L0_ffn_correction_bias,
        "up_w": np.concatenate([np.asarray(L0_ffn_up_w), shared_up]),
        "down_w": np.concatenate([np.asarray(L0_ffn_down_w), shared_down]),
    }
    nc = bacc.Bacc("TRN2", target_bir_lowering=False, num_devices=1)
    arrays, args = {}, []
    for name, a in given.items():
        a = np.ascontiguousarray(a)
        arrays[f"in_{name}"] = a
        args.append(nc.dram_tensor(f"in_{name}", a.shape, mybir.dt.from_np(a.dtype), kind="ExternalInput").ap())
    args.append(nc.dram_tensor("out_dram", (B * T, D), F32, kind="ExternalOutput").ap())
    decoder_layer(nc, *args)
    r = run_bass_kernel_spmd(nc, [arrays], core_ids=[0])
    return r.results[0]["out_dram"].reshape(B, T, D)
```
